# Optimizing a Trainium2 kernel written in Bass

```python
import numpy as np
import jax
import jax.numpy as jnp

def _softmax(x, axis=-1):
    return jax.nn.softmax(x, axis=axis)

def _gelu(x):
    return jax.nn.gelu(x, approximate=True)

def _silu(x):
    return jax.nn.silu(x)

def _sigmoid(x):
    return jax.nn.sigmoid(x)

def _layernorm(x, axis=-1, eps=1e-05):
    m = jnp.mean(x, axis=axis, keepdims=True)
    v = jnp.var(x, axis=axis, keepdims=True)
    return (x - m) / jnp.sqrt(v + eps)

def _scatter_add(tgt, idx, src, axis=0):
    return tgt.at[idx].add(src)

def _segment_sum(src, seg, n):
    return jax.ops.segment_sum(src, seg, n)
kernel_name = 'mk_gnn_resnorm_d4_gnn_r32_2a4489'

def setup_inputs(seed: int=0):
    np.random.seed(seed)
    _w = jnp.asarray

    def _rec_inputs():
        import jax
        import jax.numpy as jnp
        _gk = jax.random.key(seed)
        x = -0.0005121 + 1.001 * jax.random.normal(jax.random.fold_in(_gk, 1), (3125, 64), jnp.float32)
        _s = jax.random.randint(jax.random.fold_in(_gk, 2), (50000,), 0, 3125, jnp.int32)
        _d = jax.random.randint(jax.random.fold_in(_gk, 3), (50000,), 0, 3125, jnp.int32)
        _loop = jnp.arange(3125, dtype=jnp.int32)
        src = jnp.concatenate([_s, _d, _loop])
        dst = jnp.concatenate([_d, _s, _loop])
        _o = jnp.argsort(dst, stable=True)
        src = src[_o]
        dst = dst[_o]
        edge_attr_64 = -9.77346e-05 + 0.999888 * jax.random.normal(jax.random.fold_in(_gk, 12), (103125, 64), jnp.float32)
        edge_type_8 = jax.random.randint(jax.random.fold_in(_gk, 15), (103125,), 0, 8, jnp.int32)
        edge_weight1 = jax.random.uniform(jax.random.fold_in(_gk, 16), (103125, 1), jnp.float32, 0.0, 0.999998)
        return (x, src, dst, edge_attr_64, edge_type_8, edge_weight1)
    x, src, dst, edge_attr_64, edge_type_8, edge_weight1 = _rec_inputs()

    def _L0_gnn_setup():
        import jax, jax.numpy as jnp
        import numpy as np
        N, E, R, D_IN, D_OUT = (50000, 25000, 8, 64, 64)
        key = jax.random.key(seed)
        ks = jax.random.split(key, 8)
        feat = jax.random.normal(ks[0], (N, D_IN), dtype=jnp.float32)
        edge_src = jax.random.randint(ks[1], (E,), 0, N, dtype=jnp.int32)
        edge_dst = jax.random.randint(ks[2], (E,), 0, N, dtype=jnp.int32)
        etype = jax.random.randint(ks[3], (E,), 0, R, dtype=jnp.int32)
        attention = jax.random.uniform(ks[4], (E, 1), dtype=jnp.float32)
        weight = jax.random.normal(ks[5], (R, D_IN, D_OUT), dtype=jnp.float32) * (6.0 / (D_IN + D_OUT)) ** 0.5
        h_bias = jnp.zeros((D_OUT,), dtype=jnp.float32)
        loop_weight = jax.random.normal(ks[6], (D_IN, D_OUT), dtype=jnp.float32) * (6.0 / (D_IN + D_OUT)) ** 0.5
        return {'feat': feat, 'edge_src': edge_src, 'edge_dst': edge_dst, 'etype': etype, 'attention': attention, 'weight': weight, 'h_bias': h_bias, 'loop_weight': loop_weight}
    _L0_gnn_all = _L0_gnn_setup()
    _L0_gnn_in = {k: v for k, v in _L0_gnn_all.items() if k in ('weight', 'h_bias', 'loop_weight')}
    del _L0_gnn_all

    def _L1_gnn_setup():
        import jax, jax.numpy as jnp
        import numpy as np
        N_NODES = 3125
        N_EDGES = 50000
        D_IN = 64
        D_OUT = 64

        def _gcn_block(x, edge_index, edge_w, W, b, gamma, beta):
            n = x.shape[0]
            xw = x @ W
            loop = jnp.arange(n, dtype=edge_index.dtype)
            src = jnp.concatenate([edge_index[0], loop])
            dst = jnp.concatenate([edge_index[1], loop])
            w = jnp.concatenate([edge_w, jnp.ones((n,), dtype=x.dtype)])
            deg = jax.ops.segment_sum(w, dst, num_segments=n)
            dinv = jnp.where(deg > 0, jax.lax.rsqrt(deg), 0.0)
            norm = dinv[src] * w * dinv[dst]
            msg = xw[src] * norm[:, None]
            agg = jax.ops.segment_sum(msg, dst, num_segments=n)
            h = agg + b
            mu = jnp.mean(h, axis=-1, keepdims=True)
            var = jnp.mean(jnp.square(h - mu), axis=-1, keepdims=True)
            hn = (h - mu) * jax.lax.rsqrt(var + 1e-05) * gamma + beta
            return jax.nn.gelu(hn, approximate=False)
        key = jax.random.key(seed)
        ks = jax.random.split(key, 5)
        x = jax.random.normal(ks[0], (N_NODES, D_IN), dtype=jnp.float32)
        edge_index = jax.random.randint(ks[1], (2, N_EDGES), 0, N_NODES, dtype=jnp.int64)
        edge_attr = jax.random.uniform(ks[2], (N_EDGES, 1), dtype=jnp.float32)
        W = jax.random.normal(ks[3], (D_IN, D_OUT), dtype=jnp.float32) * (1.0 / np.sqrt(D_IN))
        b = jnp.zeros((D_OUT,), dtype=jnp.float32)
        gamma = jnp.ones((D_OUT,), dtype=jnp.float32)
        beta = jnp.zeros((D_OUT,), dtype=jnp.float32)
        return {'x': x, 'edge_index': edge_index, 'edge_attr': edge_attr, 'W': W, 'b': b, 'gamma': gamma, 'beta': beta}
    _L1_gnn_all = _L1_gnn_setup()
    _L1_gnn_in = {k: v for k, v in _L1_gnn_all.items() if k in ('W', 'b', 'gamma', 'beta')}
    del _L1_gnn_all

    def _L2_gnn_setup():
        import jax, jax.numpy as jnp
        import numpy as np
        N_NODES = 3125
        N_EDGES = 37500
        FEATS_DIM = 64
        key = jax.random.key(seed)
        k1, k2, k3 = jax.random.split(key, 3)
        feat = jax.random.normal(k1, (N_NODES, FEATS_DIM), dtype=jnp.float32)
        src = jax.random.randint(k2, (N_EDGES,), 0, N_NODES, dtype=jnp.int64)
        dst = jax.random.randint(k3, (N_EDGES,), 0, N_NODES, dtype=jnp.int64)
        return {'feat': feat, 'src': src, 'dst': dst}
    _L2_gnn_all = _L2_gnn_setup()
    _L2_gnn_in = {k: v for k, v in _L2_gnn_all.items() if k in ()}
    del _L2_gnn_all

    def _L3_gnn_setup():
        import jax, jax.numpy as jnp
        import numpy as np
        N_NODES = 50000
        N_EDGES = 25000
        EDGE_DIM = 64
        HID = 64
        key = jax.random.key(seed)
        ks = jax.random.split(key, 8)
        hidden_atom_emb = jax.random.normal(ks[0], (N_NODES, HID), dtype=jnp.float32)
        edge_emb = jax.random.normal(ks[1], (N_EDGES, EDGE_DIM), dtype=jnp.float32)
        edge_list = jax.random.randint(ks[2], (N_EDGES, 2), 0, N_NODES, dtype=jnp.int64)
        lim1 = float(np.sqrt(6.0 / (EDGE_DIM + HID)))
        W1 = jax.random.uniform(ks[3], (EDGE_DIM, HID), minval=-lim1, maxval=lim1, dtype=jnp.float32)
        b1 = jnp.zeros((HID,), dtype=jnp.float32)
        lim2 = float(np.sqrt(6.0 / (HID + HID)))
        W2 = jax.random.uniform(ks[4], (HID, HID), minval=-lim2, maxval=lim2, dtype=jnp.float32)
        b2 = jnp.zeros((HID,), dtype=jnp.float32)
        lim3 = 1.414 * float(np.sqrt(6.0 / (HID + 1)))
        linear_coef = jax.random.uniform(ks[5], (HID, 1), minval=-lim3, maxval=lim3, dtype=jnp.float32)
        return {'hidden_atom_emb': hidden_atom_emb, 'edge_emb': edge_emb, 'W1': W1, 'b1': b1, 'W2': W2, 'b2': b2, 'linear_coef': linear_coef, 'edge_list': edge_list}
    _L3_gnn_all = _L3_gnn_setup()
    _L3_gnn_in = {k: v for k, v in _L3_gnn_all.items() if k in ('W1', 'b1', 'W2', 'b2', 'linear_coef')}
    del _L3_gnn_all
    return {'x': x, 'src': src, 'dst': dst, 'edge_attr_64': edge_attr_64, 'edge_type_8': edge_type_8, 'edge_weight1': edge_weight1, 'L0_gnn_weight': _L0_gnn_in['weight'], 'L0_gnn_h_bias': _L0_gnn_in['h_bias'], 'L0_gnn_loop_weight': _L0_gnn_in['loop_weight'], 'L1_gnn_W': _L1_gnn_in['W'], 'L1_gnn_b': _L1_gnn_in['b'], 'L1_gnn_gamma': _L1_gnn_in['gamma'], 'L1_gnn_beta': _L1_gnn_in['beta'], 'L3_gnn_W1': _L3_gnn_in['W1'], 'L3_gnn_b1': _L3_gnn_in['b1'], 'L3_gnn_W2': _L3_gnn_in['W2'], 'L3_gnn_b2': _L3_gnn_in['b2'], 'L3_gnn_linear_coef': _L3_gnn_in['linear_coef']}

def reference(x, src, dst, edge_attr_64, edge_type_8, edge_weight1, L0_gnn_weight, L0_gnn_h_bias, L0_gnn_loop_weight, L1_gnn_W, L1_gnn_b, L1_gnn_gamma, L1_gnn_beta, L3_gnn_W1, L3_gnn_b1, L3_gnn_W2, L3_gnn_b2, L3_gnn_linear_coef):
    import jax
    import jax.numpy as jnp

    def _L0_gnn_ref(feat, edge_src, edge_dst, etype, attention, weight, h_bias, loop_weight):
        import jax, jax.numpy as jnp
        import numpy as np
        N, E, R, D_IN, D_OUT = (50000, 25000, 8, 64, 64)
        proj = jnp.einsum('ni,rio->rno', feat, weight)
        m = (proj[etype, edge_src] + h_bias) * attention
        agg = jax.ops.segment_sum(m, edge_dst, num_segments=feat.shape[0])
        return agg + feat @ loop_weight

    def _L1_gnn_ref(x, edge_index, edge_attr, W, b, gamma, beta):
        import jax, jax.numpy as jnp
        import numpy as np
        N_NODES = 3125
        N_EDGES = 50000
        D_IN = 64
        D_OUT = 64

        def _gcn_block(x, edge_index, edge_w, W, b, gamma, beta):
            n = x.shape[0]
            xw = x @ W
            loop = jnp.arange(n, dtype=edge_index.dtype)
            src = jnp.concatenate([edge_index[0], loop])
            dst = jnp.concatenate([edge_index[1], loop])
            w = jnp.concatenate([edge_w, jnp.ones((n,), dtype=x.dtype)])
            deg = jax.ops.segment_sum(w, dst, num_segments=n)
            dinv = jnp.where(deg > 0, jax.lax.rsqrt(deg), 0.0)
            norm = dinv[src] * w * dinv[dst]
            msg = xw[src] * norm[:, None]
            agg = jax.ops.segment_sum(msg, dst, num_segments=n)
            h = agg + b
            mu = jnp.mean(h, axis=-1, keepdims=True)
            var = jnp.mean(jnp.square(h - mu), axis=-1, keepdims=True)
            hn = (h - mu) * jax.lax.rsqrt(var + 1e-05) * gamma + beta
            return jax.nn.gelu(hn, approximate=False)
        edge_w = jnp.squeeze(edge_attr, axis=-1)
        return _gcn_block(x, edge_index, edge_w, W, b, gamma, beta)

    def _L2_gnn_ref(feat, src, dst):
        import jax, jax.numpy as jnp
        import numpy as np
        N_NODES = 3125
        N_EDGES = 37500
        FEATS_DIM = 64
        n = feat.shape[0]
        loop = jnp.arange(n, dtype=src.dtype)
        s = jnp.concatenate([src, loop])
        d = jnp.concatenate([dst, loop])
        ones = jnp.ones(s.shape[0], dtype=feat.dtype)
        deg_out = jax.ops.segment_sum(ones, s, num_segments=n)
        deg_in = jax.ops.segment_sum(ones, d, num_segments=n)
        inv_sqrt_out = jax.lax.rsqrt(jnp.maximum(deg_out, 1.0))
        inv_sqrt_in = jax.lax.rsqrt(jnp.maximum(deg_in, 1.0))
        h = feat * inv_sqrt_out[:, None]
        agg = jax.ops.segment_sum(h[s], d, num_segments=n)
        return agg * inv_sqrt_in[:, None]

    def _L3_gnn_ref(hidden_atom_emb, edge_emb, W1, b1, W2, b2, linear_coef, edge_list):
        import jax, jax.numpy as jnp
        import numpy as np
        N_NODES = 50000
        N_EDGES = 25000
        EDGE_DIM = 64
        HID = 64
        hidden_edge_emb = jnp.tanh(edge_emb @ W1 + b1) @ W2 + b2
        msg = hidden_atom_emb[edge_list[:, 1]] * hidden_edge_emb
        attn = jnp.exp(msg @ linear_coef)
        dest = edge_list[:, 0]
        n = hidden_atom_emb.shape[0]
        num = jax.ops.segment_sum(msg * attn, dest, num_segments=n)
        den = jax.ops.segment_sum(jnp.broadcast_to(attn, msg.shape), dest, num_segments=n)
        return jnp.where(den > 0, num / den, num)
    edge_index = jnp.stack([src, dst])
    edge_index_t = jnp.stack([src, dst], axis=1)
    x = _layernorm(x + _L0_gnn_ref(x, src, dst, edge_type_8, edge_weight1, L0_gnn_weight, L0_gnn_h_bias, L0_gnn_loop_weight), axis=-1)
    x = _layernorm(x + _L1_gnn_ref(x, edge_index, edge_weight1, L1_gnn_W, L1_gnn_b, L1_gnn_gamma, L1_gnn_beta), axis=-1)
    x = _layernorm(x + _L2_gnn_ref(x, src, dst), axis=-1)
    x = _layernorm(x + _L3_gnn_ref(x, edge_attr_64, L3_gnn_W1, L3_gnn_b1, L3_gnn_W2, L3_gnn_b2, L3_gnn_linear_coef, edge_index_t), axis=-1)
    return x

_drawn_inputs = setup_inputs


def setup_inputs(seed=0):
    import zlib

    import numpy as np

    out = dict(_drawn_inputs(seed))
    spreads = {'L0_gnn_h_bias': (0.0, 0.1),
     'L1_gnn_b': (0.0, 0.1),
     'L1_gnn_gamma': (1.0, 0.2),
     'L1_gnn_beta': (0.0, 0.1),
     'L3_gnn_b1': (0.0, 0.1),
     'L3_gnn_b2': (0.0, 0.1)}
    factors = {}
    for name, (base, spread) in spreads.items():
        noise = np.random.default_rng([zlib.crc32(name.encode()), seed]).standard_normal(out[name].shape)
        drawn = base * np.exp(spread * noise) if base else spread * noise
        out[name] = jnp.asarray(drawn.astype(out[name].dtype))
    for name, factor in factors.items():
        out[name] = (out[name] * factor).astype(out[name].dtype)
    return out
```

```python
import concourse.bass as bass
from concourse import mybir

N = 3125
F = 64
E = 103125
R = 8
P = 128
NT = -(-N // P)
TAIL = N - (NT - 1) * P
J = 15
BE = P * J
NB = -(-E // BE)
assert NB % 2 == 0
LAST = E - BE
REPEATED = ((NB - 1) * BE - LAST) // J
assert REPEATED * J == (NB - 1) * BE - LAST
WINDOW = 128
W1 = F + 1
BANK_TILES = [(0, 7), (7, 14), (14, 21), (21, NT)]
PAIRS = [(0, 1, 2), (3, 4, 5), (6, 7)]
EPS = 1e-5

F32 = mybir.dt.float32
I32 = mybir.dt.int32
ALU = mybir.AluOpType
ACT = mybir.ActivationFunctionType
AX = mybir.AxisListType.X
GNN0, GNN1, GNN2, GNN3 = range(4)


def build(nc, A, out):
    def sb(name, shape, dt=F32):
        return nc.alloc_sbuf_tensor(name, list(shape), dt)

    def sem(name):
        return nc.alloc_semaphore(name)

    table = [nc.dram_tensor("table_typed", (N * R, F), F32, kind="Internal").ap(),
             nc.dram_tensor("table_gcn", (N, F), F32, kind="Internal").ap(),
             nc.dram_tensor("table_sym", (N, F), F32, kind="Internal").ap(),
             nc.dram_tensor("table_attn", (N, F), F32, kind="Internal").ap()]

    iota_row = sb("iota_row", [P, P])
    iota_tile = sb("iota_tile", [P, NT])
    row_no = sb("row_no", [P, 1])
    ident = sb("ident", [P, P])
    ones = sb("ones", [P, P])
    zero_mat = sb("zero_mat", [P, P])

    src_i = sb("src_i", [P, NB * J], I32)
    dst_i = sb("dst_i", [P, NB * J], I32)
    type_i = sb("type_i", [P, NB * J], I32)
    typed_i = sb("typed_i", [P, NB * J], I32)
    weight = sb("weight", [P, NB * J])
    tmp_i = sb("tmp_i", [P, NB * J], I32)
    rel = sb("rel", [P, NB * J])
    src_lo = sb("src_lo", [P, NB * J])
    src_hi = sb("src_hi", [P, NB * J])
    far_lo = sb("far_lo", [P, NB * J])
    far_hi = sb("far_hi", [P, NB * J])
    outside = sb("outside", [P, NB * J])
    inside = sb("inside", [P, NB * J])
    first_f = sb("first_f", [1, NB])
    first = sb("first", [P, NB])
    win_i = sb("win_i", [P, NB], I32)
    win_t = sb("win_t", [P, NB], I32)
    win_lo = sb("win_lo", [P, NB])
    win_hi = sb("win_hi", [P, NB])
    win_mask = sb("win_mask", [P, NB, NT])
    any_col = sb("any_col", [P, 1])
    any_i = sb("any_i", [1, 1], I32)

    x = sb("x", [P, NT, F])
    xc = sb("xc", [P, NT, F])
    tmp = sb("tmp", [P, NT, F])
    agg = sb("agg", [P, NT, W1])
    seed = sb("seed", [P, NT, W1])
    xT = sb("xT", [F, NT * P])
    stat = sb("stat", [P, NT])
    stat2 = sb("stat2", [P, NT])
    dinv = sb("dinv", [P, NT])
    deg_out = sb("deg_out", [P, NT])
    stage = sb("stage", [P, 2, R * F])

    w_types = sb("w_types", [F, R, F])
    w_loop = sb("w_loop", [F, W1])
    w_gcn = sb("w_gcn", [F, F])
    h_bias = sb("h_bias", [P, F])
    g_bias = sb("g_bias", [P, F])
    gamma = sb("gamma", [P, F])
    beta = sb("beta", [P, F])
    mlp1 = sb("mlp1", [P, P])
    mlp2 = sb("mlp2", [P, P])
    mlp_b1 = sb("mlp_b1", [P, 1])
    mlp_b2 = sb("mlp_b2", [P, F])
    coef = sb("coef", [P, F])

    idx = sb("idx", [P, 2, J], I32)
    rows = [sb(f"rows{s}", [P, J, W1]) for s in range(2)]
    msg = [sb(f"msg{s}", [P, J, W1]) for s in range(2)]
    hot = [sb(f"hot{s}", [P, J, P]) for s in range(2)]
    attn = sb("attn", [P, 2, J])
    logit = sb("logit", [P, 2, J])
    prod = sb("prod", [P, J, F])
    mlp_out = [sb(f"mlp_out{s}", [P, J, F]) for s in range(2)]
    ea = [sb(f"ea{s}", [P, J * F]) for s in range(2)]
    eaT = [sb(f"eaT{u}", [P, 3 * P]) for u in range(3)]
    hidT = [sb(f"hidT{u}", [P, 3 * P]) for u in range(3)]
    spread = [sb(f"spread{s}", [P, NT, W1]) for s in range(2)]
    spread_hot = sb("spread_hot", [P, 2, P])
    far_mask = sb("far_mask", [P, 2, NT])
    src_hot = [sb(f"src_hot{s}", [P, J, P], mybir.dt.bfloat16) for s in range(2)]
    src_tile = [sb(f"src_tile{s}", [P, J, NT], mybir.dt.bfloat16) for s in range(2)]

    sums = [nc.alloc_psum_tensor(f"sums{g}", [P, 512], F32) for g in range(4)]
    bank_t = nc.alloc_psum_tensor("bank_t", [P, 512], F32)
    bank_h = nc.alloc_psum_tensor("bank_h", [P, 512], F32)
    wide = [nc.alloc_psum_tensor(f"wide{g}", [P, 512], F32) for g in range(2)]
    part = [bank_t[:, 384:384 + W1], bank_h[:, 384:384 + W1]]
    degs = wide[0][:, 0:NT]

    src_in, dst_in, x_in, wts_in, w_in = sem("src_in"), sem("dst_in"), sem("x_in"), sem("wts_in"), sem("w_in")
    consts = sem("consts")
    zeroed = sem("zeroed")
    dve_step = sem("dve_step")
    pool_copied = sem("pool_copied")
    first_cast = sem("first_cast")
    first_bc = sem("first_bc")
    any_sum = sem("any_sum")
    any_col_ready = sem("any_col_ready")
    flag_ready = sem("flag_ready")
    prep_ready = sem("prep_ready")
    idx0_ready = sem("idx0_ready")
    x_ready = sem("x_ready")
    tr_done = sem("tr_done")
    tr_copied = sem("tr_copied")
    prod_done = sem("prod_done")
    prod_used = sem("prod_used")
    stage_out = [sem("stage_out0"), sem("stage_out1")]
    seed_ready = sem("seed_ready")
    table_ready = sem("table_ready")
    table_out = sem("table_out")
    out_done = sem("out_done")
    src_hot_ready = sem("src_hot_ready")
    src_hot_used = sem("src_hot_used")
    root_in, root_done = sem("root_in"), sem("root_done")
    gelu_in, gelu_done = sem("gelu_in"), sem("gelu_done")

    class Sems:

        def __init__(self, way):
            self.rows_in = [sem(f"{way}_rows_in{s}") for s in range(2)]
            self.ea_in = [sem(f"{way}_ea_in{s}") for s in range(2)]
            self.idx_staged = sem(f"{way}_idx_staged")
            self.main_done = sem(f"{way}_main_done")
            self.hot_ready = sem(f"{way}_hot_ready")
            self.spread_ready = sem(f"{way}_spread_ready")
            self.merged = sem(f"{way}_merged")
            self.mask_done = sem(f"{way}_mask_done")
            self.msg_done = sem(f"{way}_msg_done")
            self.prod_ready = sem(f"{way}_prod_ready")
            self.logit_ready = sem(f"{way}_logit_ready")
            self.attn_ready = sem(f"{way}_attn_ready")
            self.t_ready = sem(f"{way}_t_ready")
            self.t_copied = sem(f"{way}_t_copied")
            self.h_ready = sem(f"{way}_h_ready")
            self.hid_ready = sem(f"{way}_hid_ready")
            self.unit_done = sem(f"{way}_unit_done")
            self.mlp_copied = sem(f"{way}_mlp_copied")

    near, far, attend = Sems("near"), Sems("far"), Sems("attend")
    SLOTS = 2
    FAR_SLOTS = 2 * J

    def edges(a):
        return a[0:(NB - 1) * BE].rearrange("(b p j) -> p b j", p=P, j=J)

    def blocks(eng, body, peel):
        if peel:
            with eng.Fori(0, NB // 2 - 1) as i:
                body(i, False)
            body(NB // 2 - 1, True)
        else:
            with eng.Fori(0, NB // 2) as i:
                body(i, False)

    def far_way(eng, run):
        count = eng.value_load(any_i[0:1, 0:1], min_val=0, max_val=NB * BE)
        with eng.If(count > 0):
            run()

    with nc.Block() as block:

        @block.sync
        def _(sp):
            flat_w = A["edge_weight1"].rearrange("e o -> (e o)")
            for t, a, s in ((src_i, A["src"], src_in), (type_i, A["edge_type_8"], src_in),
                            (dst_i, A["dst"], dst_in)):
                sp.dma_start(t[:, 0:(NB - 1) * J].rearrange("p (b j) -> p b j", j=J), edges(a)).then_inc(s, 16)
                sp.dma_start(t[:, (NB - 1) * J:], a[LAST:E].rearrange("(p j) -> p j", j=J)).then_inc(s, 16)
            sp.dma_start(weight[:, 0:(NB - 1) * J].rearrange("p (b j) -> p b j", j=J), edges(flat_w))\
              .then_inc(w_in, 16)
            sp.dma_start(weight[:, (NB - 1) * J:], flat_w[LAST:E].rearrange("(p j) -> p j", j=J)).then_inc(w_in, 16)

            for t in range(NT):
                n = P if t < NT - 1 else TAIL
                sp.wait_ge(table_ready, t + 1)
                sp.dma_start(table[GNN0][t * P * R:(t * P + n) * R, :].rearrange("(p r) f -> p (r f)", r=R),
                             stage[0:n, t % 2, :]).then_inc(stage_out[t % 2], 16)

            for layer, source in ((GNN1, seed), (GNN2, seed), (GNN3, x)):
                sp.wait_ge(table_ready, NT + layer)
                sp.dma_start(table[layer][0:(NT - 1) * P, :].rearrange("(t p) f -> p t f", p=P),
                             source[:, 0:NT - 1, 0:F]).then_inc(table_out, 16)
                sp.dma_start(table[layer][(NT - 1) * P:N, :], source[0:TAIL, NT - 1, 0:F]).then_inc(table_out, 16)

            def attributes(S):
                def load(i, s, start):
                    sp.wait_ge(S.unit_done, 3 * (2 * i + s) + 3)
                    sp.dma_start(ea[s][:, :], A["edge_attr_64"][bass.ds(start, BE), :]
                                 .rearrange("(p j) f -> p (j f)", j=J)).then_inc(S.ea_in[s], 16)

                def body(i, last):
                    load(i, 0, i * (2 * BE))
                    load(i, 1, LAST if last else i * (2 * BE) + BE)
                blocks(sp, body, True)

            attributes(attend)

            sp.wait_ge(table_ready, NT + 4)
            sp.dma_start(out[0:(NT - 1) * P, :].rearrange("(t p) f -> p t f", p=P), x[:, 0:NT - 1, :])\
              .then_inc(out_done, 16)
            sp.dma_start(out[(NT - 1) * P:N, :], x[0:TAIL, NT - 1, :]).then_inc(out_done, 16)
            sp.wait_ge(out_done, 32)

        @block.gpsimd
        def _(pool):
            pool.iota(iota_row[:, :], pattern=[[1, P]], base=0, channel_multiplier=0,
                      allow_small_or_imprecise_dtypes=True).then_inc(consts, 1)
            pool.iota(iota_tile[:, :], pattern=[[1, NT]], base=0, channel_multiplier=0,
                      allow_small_or_imprecise_dtypes=True).then_inc(consts, 1)
            pool.iota(row_no[:, :], pattern=[[0, 1]], base=0, channel_multiplier=1,
                      allow_small_or_imprecise_dtypes=True).then_inc(consts, 1)

            def gathers(layer, S, v0):
                index = {GNN0: typed_i, GNN1: src_i, GNN2: src_i, GNN3: dst_i}[layer]

                def body(i, last):
                    for s in range(2):
                        v = 2 * i + s
                        if layer == GNN3:
                            pool.wait_ge(S.msg_done, v + 1)
                        elif S is near:
                            pool.wait_ge(S.main_done, v0 + v + 1)
                        else:
                            pool.wait_ge(S.merged, (v0 + v) * J + J)
                        pool.tensor_copy(idx[:, s, :], index[:, bass.ds(v * J, J)]).then_inc(S.idx_staged, 1)
                        pool.wait_ge(S.idx_staged, 1)
                        pool.sem_clear(S.idx_staged)
                        for j in range(J):
                            pool.indirect_dma_start(
                                out=rows[s][:, j, 0:F], out_offset=None, in_=table[layer][:, :],
                                in_offset=bass.IndirectOffsetOnAxis(ap=idx[:, s, j:j + 1], axis=0),
                            ).then_inc(S.rows_in[s], 16)
                blocks(pool, body, False)

            pool.wait_ge(idx0_ready, 1)
            for layer in range(4):
                if layer == GNN0:
                    pool.wait_ge(stage_out[0], 16 * ((NT + 1) // 2))
                    pool.wait_ge(stage_out[1], 16 * (NT // 2))
                else:
                    pool.wait_ge(table_out, 32 * layer)
                if layer == GNN3:
                    gathers(layer, attend, 0)
                    continue
                gathers(layer, near, layer * NB)
                if layer == GNN0:
                    pool.wait_ge(flag_ready, 1)
                far_way(pool, lambda: gathers(layer, far, layer * NB))

        @block.scalar
        def _(act):
            act.dma_start(x[:, 0:NT - 1, :], A["x"][0:(NT - 1) * P, :].rearrange("(t p) f -> p t f", p=P))\
               .then_inc(x_in, 16)
            act.wait_ge(zeroed, 1)
            act.dma_start(x[0:TAIL, NT - 1, :], A["x"][(NT - 1) * P:N, :]).then_inc(x_in, 16)
            act.dma_start(w_types[:, :, :], A["L0_gnn_weight"].rearrange("r i o -> i r o")).then_inc(wts_in, 16)
            act.dma_start(w_loop[:, 0:F], A["L0_gnn_loop_weight"]).then_inc(wts_in, 16)
            act.dma_start(w_gcn[:, :], A["L1_gnn_W"]).then_inc(wts_in, 16)
            for t, name in ((h_bias, "L0_gnn_h_bias"), (g_bias, "L1_gnn_b"), (gamma, "L1_gnn_gamma"),
                            (beta, "L1_gnn_beta"), (mlp_b2, "L3_gnn_b2")):
                act.dma_start(t[:, :], A[name].partition_broadcast(P)).then_inc(wts_in, 16)
            act.dma_start(coef[:, :], A["L3_gnn_linear_coef"].rearrange("f o -> (f o)").partition_broadcast(P))\
               .then_inc(wts_in, 16)
            for h in range(2):
                q = slice(h * F, (h + 1) * F)
                act.dma_start(mlp1[q, q], A["L3_gnn_W1"]).then_inc(wts_in, 16)
                act.dma_start(mlp2[q, q], A["L3_gnn_W2"]).then_inc(wts_in, 16)
                act.dma_start(mlp_b1[q, :], A["L3_gnn_b1"].rearrange("(f o) -> f o", o=1)).then_inc(wts_in, 16)

            def copy_transposed(base):
                for g in range(-(-NT // 4)):
                    n = min(4, NT - 4 * g) * P
                    act.wait_ge(tr_done, base + g + 1)
                    act.activation(xT[:, 4 * g * P:4 * g * P + n], (bank_t, bank_h)[g % 2][0:F, 0:n], ACT.Copy)\
                       .then_inc(tr_copied, 1)

            roots = [0]

            def root(a):
                roots[0] += 1
                act.wait_ge(root_in, roots[0])
                act.activation(a[:, :], a[:, :], ACT.Sqrt).then_inc(root_done, 1)

            copy_transposed(0)
            root(stat2)
            copy_transposed(-(-NT // 4))
            root(dinv)
            root(stat2)
            act.wait_ge(gelu_in, 1)
            act.activation(xc[:, :, :], tmp[:, :, :], ACT.Gelu).then_inc(gelu_done, 1)
            root(stat2)
            root(stat)
            root(stat)
            root(stat2)

            def mlp(S):
                def units(v):
                    for u, pairs in enumerate(PAIRS):
                        n = len(pairs) * P
                        act.wait_ge(S.t_ready, 3 * v + u + 1)
                        act.activation(eaT[u][:, 0:n], bank_t[:, 0:n], ACT.Copy).then_inc(S.t_copied, 1)
                        act.wait_ge(S.h_ready, 3 * v + u + 1)
                        act.wait_ge(S.unit_done, 3 * v + u + 4)
                        act.activation(hidT[u][:, 0:n], bank_h[:, 0:n], ACT.Tanh, bias=mlp_b1[:, 0:1])\
                           .then_inc(S.hid_ready, 1)

                def body(i, last):
                    for s in range(2):
                        v = 2 * i + s
                        if not (last and s == 1):
                            units(v + 1)
                        act.wait_ge(S.logit_ready, v + 1)
                        act.activation(attn[:, s, :], logit[:, s, :], ACT.Exp).then_inc(S.attn_ready, 1)
                units(0)
                blocks(act, body, True)

            act.wait_ge(wts_in, 16 * 15)
            mlp(attend)
            root(stat2)

        @block.tensor
        def _(pe):
            pe.sem_inc(near.main_done, SLOTS)
            pe.sem_inc(near.merged, SLOTS)
            pe.sem_inc(far.merged, FAR_SLOTS)
            pe.sem_inc(src_hot_used, SLOTS)
            pe.sem_inc(attend.merged, FAR_SLOTS)
            pe.sem_inc(attend.unit_done, SLOTS * len(PAIRS))

            def transpose_nodes(base):
                for g in range(-(-NT // 4)):
                    if g >= 2:
                        pe.wait_ge(tr_copied, base + g - 1)
                    for k in range(min(4, NT - 4 * g)):
                        last = pe.transpose((bank_t, bank_h)[g % 2][0:F, k * P:(k + 1) * P], x[:, 4 * g + k, :], ident[:, :])
                    last.then_inc(tr_done, 1)

            def start_sums(lhsT):
                for g, (t0, t1) in enumerate(BANK_TILES):
                    for t in range(t0, t1):
                        lhs, rhs = lhsT(t)
                        pe.matmul(sums[g][:, (t - t0) * W1:(t - t0 + 1) * W1], lhs, rhs,
                                  start=(t == t0), stop=True, skip_group_check=True)

            def merge(slot, done):
                for g, (t0, t1) in enumerate(BANK_TILES):
                    last = pe.matmul(sums[g][:, 0:(t1 - t0) * W1], spread_hot[:, slot, :],
                                     spread[slot][:, t0:t1, :].rearrange("p t f -> p (t f)"),
                                     start=False, stop=True, skip_group_check=True)
                last.then_inc(done, 1)

            def mlp_units(S, v, k, s):
                pe.wait_ge(S.ea_in[s], 16 * (k + 1))
                for u, pairs in enumerate(PAIRS):
                    n = len(pairs) * P
                    pe.wait_ge(S.t_copied, 3 * v + u + 1)
                    for c, q in enumerate(pairs):
                        at = min(2 * q, J - 2) * F
                        last = pe.transpose(bank_t[:, c * P:(c + 1) * P], ea[s][:, at:at + P], ident[:, :])
                    last.then_inc(S.t_ready, 1)
                    pe.wait_ge(S.t_copied, 3 * v + u + 2)
                    pe.matmul(bank_h[:, 0:n], mlp1[:, :], eaT[u][:, 0:n], start=True, stop=True)\
                      .then_inc(S.h_ready, 1)
                    pe.wait_ge(S.hid_ready, 3 * v + u + 1)
                    if u == 0:
                        pe.wait_ge(S.mlp_copied, v + 1)
                    for c, q in enumerate(pairs):
                        at = min(2 * q, J - 2) * F
                        last = pe.matmul(wide[at // 512][:, at % 512:at % 512 + P], hidT[u][:, c * P:(c + 1) * P],
                                         mlp2[:, :], start=True, stop=True)
                    last.then_inc(S.unit_done, 1)

            def near_blocks(layer, v0):
                S = near

                def body(i, last):
                    for s in range(2):
                        v = 2 * i + s
                        if layer == GNN1:
                            pe.wait_ge(src_hot_ready, v + 1)
                            for j in range(J):
                                mm = pe.matmul(degs, src_hot[s][:, j, :], src_tile[s][:, j, :],
                                               start=False, stop=True, skip_group_check=True)
                            mm.then_inc(src_hot_used, 1)
                        pe.wait_ge(S.hot_ready, v0 + v + 1)
                        pe.wait_ge(S.rows_in[s], (i + v0 // 2) * (16 * J) + 16 * J)
                        for j in range(J):
                            mm = pe.matmul(part[s], hot[s][:, j, :], rows[s][:, j, :], start=(j == 0), stop=(j == J - 1))
                        mm.then_inc(S.main_done, 1)
                        pe.wait_ge(S.spread_ready, v0 + v + 1)
                        merge(s, S.merged)
                blocks(pe, body, False)

            def far_blocks(layer, v0, S=far):
                def body(i, last):
                    for s in range(2):
                        v = 2 * i + s
                        if layer == GNN3 and not (last and s == 1):
                            mlp_units(S, v + 1, i + s, 1 - s)
                        for j in range(J):
                            pe.wait_ge(S.spread_ready, (v0 + v) * J + j + 1)
                            merge((s + j) % 2, S.merged)
                if layer == GNN3:
                    mlp_units(S, 0, 0, 0)
                blocks(pe, body, layer == GNN3)

            pe.wait_ge(x_ready, 1)
            transpose_nodes(0)
            pe.wait_ge(wts_in, 16 * 15)
            pe.wait_ge(tr_copied, -(-NT // 4))
            for t in range(NT):
                pe.wait_ge(prod_used, t + 1)
                pe.matmul(wide[t % 2][:, :], xT[:, t * P:(t + 1) * P], w_types[:, :, :].rearrange("i r o -> i (r o)"),
                          start=True, stop=True).then_inc(prod_done, 1)
            start_sums(lambda t: (xT[:, t * P:(t + 1) * P], w_loop[:, :]))
            pe.wait_ge(first_cast, 1)
            pe.matmul(wide[0][:, 0:NB], ones[0:1, :], first_f[0:1, :], start=True, stop=True).then_inc(first_bc, 1)
            pe.wait_ge(any_col_ready, 1)
            pe.matmul(wide[1][0:1, 0:1], any_col[:, 0:1], ones[:, 0:1], start=True, stop=True).then_inc(any_sum, 1)

            near_blocks(GNN0, 0)
            pe.wait_ge(flag_ready, 1)
            far_way(pe, lambda: far_blocks(GNN0, 0))

            pe.wait_ge(x_ready, 2)
            transpose_nodes(-(-NT // 4))
            pe.wait_ge(tr_copied, 2 * -(-NT // 4))
            for g in range(-(-NT // 4)):
                pe.wait_ge(prod_used, NT + g + 1)
                for k in range(min(4, NT - 4 * g)):
                    t = 4 * g + k
                    mm = pe.matmul(wide[g % 2][:, k * F:(k + 1) * F], xT[:, t * P:(t + 1) * P], w_gcn[:, :],
                                   start=True, stop=True)
                mm.then_inc(prod_done, 1)
            pe.wait_ge(seed_ready, 1)
            pe.matmul(degs, zero_mat[:, :], iota_tile[:, :], start=True, stop=True, skip_group_check=True)
            start_sums(lambda t: (ident[:, :], seed[:, t, :]))
            near_blocks(GNN1, NB)
            far_way(pe, lambda: far_blocks(GNN1, NB))

            pe.wait_ge(seed_ready, 2)
            start_sums(lambda t: (ident[:, :], seed[:, t, :]))
            near_blocks(GNN2, 2 * NB)
            far_way(pe, lambda: far_blocks(GNN2, 2 * NB))

            pe.wait_ge(seed_ready, 3)
            start_sums(lambda t: (ident[:, :], seed[:, t, :]))
            far_blocks(GNN3, 0, attend)

        @block.vector
        def _(dve):
            steps = [0]

            def step(ins):
                steps[0] += 1
                ins.then_inc(dve_step, 1)
                dve.wait_ge(dve_step, steps[0])

            def rowwise(a):
                return a.unsqueeze(2).to_broadcast([P, NT, F])

            def featurewise(a):
                return a.unsqueeze(1).to_broadcast([P, NT, F])

            roots = [0]

            def inverse_root(a):
                roots[0] += 1
                step(dve.reciprocal(a[:, :], a[:, :]))
                dve.sem_inc(root_in, 1)
                dve.wait_ge(root_done, roots[0])

            def layer_norm(src, dst, mean=stat, var=stat2):
                step(dve.tensor_reduce(mean[:, :], src, axis=AX, op=ALU.add))
                step(dve.tensor_scalar(mean[:, :], mean[:, :], 1.0 / F, None, ALU.mult))
                step(dve.tensor_tensor(xc[:, :, :], src, rowwise(mean[:, :]), ALU.subtract))
                step(dve.tensor_tensor(dst, xc[:, :, :], xc[:, :, :], ALU.mult))
                step(dve.tensor_reduce(var[:, :], dst, axis=AX, op=ALU.add))
                step(dve.tensor_scalar(var[:, :], var[:, :], 1.0 / F, EPS, ALU.mult, ALU.add))
                inverse_root(var)
                step(dve.tensor_tensor(dst, xc[:, :, :], rowwise(var[:, :]), ALU.mult))

            def read_sums(layer, all_near):
                if layer == GNN3:
                    far_blocks(layer, 0, attend)
                else:
                    dve.wait_ge(near.merged, SLOTS + all_near)
                    far_way(dve, lambda: far_blocks(layer, layer * NB, far))
                for g, (t0, t1) in enumerate(BANK_TILES):
                    last = dve.tensor_copy(agg[:, t0:t1, :], sums[g][:, 0:(t1 - t0) * W1].rearrange("p (t f) -> p t f", f=W1))
                step(last)

            def edge_scale(layer, s, j, c):
                if layer in (GNN0, GNN1):
                    return weight[:, bass.ds(c, 1)]
                return attn[:, s, j:j + 1] if layer == GNN3 else None

            def one_hot(out_, numbers, value, scale):
                if scale is None:
                    return dve.tensor_scalar(out_, numbers, value, None, ALU.is_equal)
                return dve.tensor_scalar(out_, numbers, value, scale, ALU.is_equal, ALU.mult)

            def messages(S, v, k, s, first_free):
                dve.wait_ge(S.unit_done, 3 * v + 9)
                for g in range(2):
                    n = 8 if g == 0 else J - 8
                    mm = dve.tensor_tensor(mlp_out[s][:, 8 * g:8 * g + n, :],
                                           wide[g][:, 0:n * F].rearrange("p (j f) -> p j f", f=F),
                                           mlp_b2[:, :].unsqueeze(1).to_broadcast([P, n, F]), ALU.add)
                mm.then_inc(S.mlp_copied, 1)
                dve.wait_ge(S.mlp_copied, v + 2)
                dve.wait_ge(S.rows_in[s], k)
                first_free()
                dve.tensor_tensor(msg[s][:, :, 0:F], rows[s][:, :, 0:F], mlp_out[s][:, :, :], ALU.mult)\
                   .then_inc(S.msg_done, 1)
                dve.wait_ge(S.msg_done, v + SLOTS + 1)
                dve.tensor_tensor(prod[:, :, :], msg[s][:, :, 0:F],
                                  coef[:, :].unsqueeze(1).to_broadcast([P, J, F]), ALU.mult).then_inc(S.prod_ready, 1)
                dve.wait_ge(S.prod_ready, v + 1)
                dve.tensor_reduce(logit[:, s, :], prod[:, :, :], axis=AX, op=ALU.add).then_inc(S.logit_ready, 1)

            def near_blocks(layer, v0):
                S = near

                def body(i, last):
                    for s in range(2):
                        v = 2 * i + s
                        if layer == GNN1:
                            dve.wait_ge(src_hot_used, v + 1)
                            dve.tensor_tensor(src_hot[s][:, :, :], iota_row[:, :].unsqueeze(1).to_broadcast([P, J, P]),
                                              src_lo[:, bass.ds(v * J, J)].unsqueeze(2).to_broadcast([P, J, P]), ALU.is_equal)
                            dve.tensor_tensor(src_tile[s][:, :, :], iota_tile[:, :].unsqueeze(1).to_broadcast([P, J, NT]),
                                              src_hi[:, bass.ds(v * J, J)].unsqueeze(2).to_broadcast([P, J, NT]), ALU.is_equal)\
                               .then_inc(src_hot_ready, 1)
                        dve.wait_ge(S.main_done, v0 + v + 1)
                        for j in range(J):
                            mm = one_hot(hot[s][:, j, :], iota_row[:, :], rel[:, bass.ds(v * J + j, 1)],
                                         edge_scale(layer, s, j, v * J + j))
                        mm.then_inc(S.hot_ready, 1)
                        dve.wait_ge(S.merged, v0 + v + 1)
                        one_hot(spread_hot[:, s, :], iota_row[:, :], win_lo[:, bass.ds(v, 1)], None)
                        dve.wait_ge(S.main_done, v0 + v + SLOTS + 1)
                        dve.tensor_tensor(spread[s][:, :, :], part[s].unsqueeze(1).to_broadcast([P, NT, W1]),
                                          win_mask[:, bass.ds(v, 1), :].rearrange("p b t -> p (b t)").unsqueeze(2)
                                          .to_broadcast([P, NT, W1]), ALU.mult).then_inc(S.spread_ready, 1)
                blocks(dve, body, False)

            def far_blocks(layer, v0, S):
                lo, hi = (src_lo, src_hi) if layer == GNN3 else (far_lo, far_hi)

                def body(i, last):
                    for s in range(2):
                        v = 2 * i + s
                        landed = (i + v0 // 2) * (16 * J) + 16 * J
                        if layer == GNN3:
                            messages(S, v, landed, s, lambda: dve.wait_ge(S.merged, (v0 + v) * J + J))
                            dve.wait_ge(S.attn_ready, v + 1)
                        else:
                            dve.wait_ge(S.rows_in[s], landed)
                        data = msg if layer == GNN3 else rows
                        for j in range(J):
                            q = (s + j) % 2
                            g = (v0 + v) * J + j
                            dve.wait_ge(S.merged, g + FAR_SLOTS - 1)
                            dve.tensor_scalar(far_mask[:, q, :], iota_tile[:, :], hi[:, bass.ds(v * J + j, 1)],
                                              None, ALU.is_equal).then_inc(S.mask_done, 1)
                            one_hot(spread_hot[:, q, :], iota_row[:, :], lo[:, bass.ds(v * J + j, 1)],
                                    edge_scale(layer, s, j, v * J + j))
                            dve.wait_ge(S.mask_done, g + 1)
                            dve.tensor_tensor(spread[q][:, :, :],
                                              data[s][:, j, :].unsqueeze(1).to_broadcast([P, NT, W1]),
                                              far_mask[:, q, :].unsqueeze(2).to_broadcast([P, NT, W1]), ALU.mult)\
                               .then_inc(S.spread_ready, 1)
                blocks(dve, body, layer == GNN3)
                dve.wait_ge(S.merged, FAR_SLOTS + (v0 + NB) * J)

            dve.sem_inc(attend.msg_done, SLOTS)
            dve.sem_inc(attend.mlp_copied, 1)
            dve.sem_inc(attend.t_copied, 1)
            dve.sem_inc(prod_used, 2)
            dve.memset(x[:, NT - 1, :], 0.0)
            dve.memset(mlp1[:, :], 0.0)
            dve.memset(mlp2[:, :], 0.0).then_inc(zeroed, 1)
            dve.memset(w_loop[:, F:W1], 0.0)
            dve.memset(zero_mat[:, :], 0.0)
            for s in range(2):
                dve.memset(rows[s][:, :, F:W1], 1.0)
                dve.memset(msg[s][:, :, F:W1], 1.0)
            step(dve.memset(ones[:, :], 1.0))
            dve.wait_ge(consts, 3)
            step(dve.tensor_scalar(ident[:, :], iota_row[:, :], row_no[:, 0:1], None, ALU.is_equal))
            dve.wait_ge(src_in, 64)
            step(dve.tensor_scalar(tmp_i[:, :], src_i[:, :], float(R), None, ALU.mult))
            dve.tensor_tensor(typed_i[:, :], tmp_i[:, :], type_i[:, :], ALU.add).then_inc(idx0_ready, 1)
            dve.wait_ge(x_in, 32)
            dve.wait_ge(idx0_ready, 1)
            dve.sem_inc(x_ready, 1)

            dve.wait_ge(wts_in, 16 * 15)
            for t in range(NT):
                dve.wait_ge(prod_done, t + 1)
                if t >= 2:
                    dve.wait_ge(stage_out[t % 2], 16 * (t // 2))
                dve.tensor_tensor(stage[:, t % 2, :].rearrange("p (r f) -> p r f", f=F),
                                  wide[t % 2][:, :].rearrange("p (r f) -> p r f", f=F),
                                  h_bias[:, :].unsqueeze(1).to_broadcast([P, R, F]), ALU.add).then_inc(prod_used, 1)
                dve.wait_ge(prod_used, t + 3)
                dve.sem_inc(table_ready, 1)

            dve.wait_ge(dst_in, 32)
            step(dve.tensor_copy(first_f[0:1, :], dst_i[0:1, :].rearrange("p (b j) -> p b j", j=J)[:, :, 0]))
            dve.sem_inc(first_cast, 1)
            dve.wait_ge(first_bc, 1)
            step(dve.tensor_copy(first[:, :], wide[0][:, 0:NB]))
            step(dve.tensor_scalar(win_i[:, :], first[:, :], row_no[:, 0:1], None, ALU.add))
            per_block = first[:, :].unsqueeze(2).to_broadcast([P, NB, J])
            step(dve.tensor_tensor(rel[:, :].rearrange("p (b j) -> p b j", j=J),
                                   dst_i[:, :].rearrange("p (b j) -> p b j", j=J), per_block, ALU.subtract))
            step(dve.tensor_single_scalar(win_t[:, :], win_i[:, :], P - 1, ALU.bitwise_and))
            step(dve.tensor_copy(win_lo[:, :], win_t[:, :]))
            step(dve.tensor_single_scalar(win_t[:, :], win_i[:, :], 7, ALU.arith_shift_right))
            step(dve.tensor_copy(win_hi[:, :], win_t[:, :]))
            step(dve.tensor_tensor(win_mask[:, :, :], iota_tile[:, :].unsqueeze(1).to_broadcast([P, NB, NT]),
                                   win_hi[:, :].unsqueeze(2).to_broadcast([P, NB, NT]), ALU.is_equal))
            step(dve.tensor_scalar(inside[:, :], rel[:, :], 0.0, None, ALU.is_ge))
            step(dve.tensor_scalar(outside[:, :], rel[:, :], float(WINDOW), None, ALU.is_lt))
            step(dve.tensor_tensor(inside[:, :], inside[:, :], outside[:, :], ALU.mult))
            step(dve.tensor_scalar(outside[:, :], inside[:, :], -1.0, 1.0, ALU.mult, ALU.add))
            step(dve.memset(outside[0:REPEATED, (NB - 1) * J:], 0.0))
            step(dve.tensor_reduce(any_col[:, :], outside[:, :], axis=AX, op=ALU.add))
            dve.sem_inc(any_col_ready, 1)
            step(dve.tensor_scalar(rel[:, :], rel[:, :], 1.0, None, ALU.add))
            step(dve.tensor_tensor(rel[:, :], rel[:, :], inside[:, :], ALU.mult))
            step(dve.tensor_scalar(rel[:, :], rel[:, :], -1.0, None, ALU.add))
            step(dve.memset(rel[0:REPEATED, (NB - 1) * J:], -1.0))
            step(dve.tensor_single_scalar(tmp_i[:, :], dst_i[:, :], P - 1, ALU.bitwise_and))
            step(dve.tensor_copy(far_lo[:, :], tmp_i[:, :]))
            step(dve.tensor_single_scalar(tmp_i[:, :], dst_i[:, :], 7, ALU.arith_shift_right))
            step(dve.tensor_copy(far_hi[:, :], tmp_i[:, :]))
            step(dve.tensor_scalar(far_hi[:, :], far_hi[:, :], 1.0, None, ALU.add))
            step(dve.tensor_tensor(far_hi[:, :], far_hi[:, :], outside[:, :], ALU.mult))
            step(dve.tensor_scalar(far_hi[:, :], far_hi[:, :], -1.0, None, ALU.add))
            step(dve.tensor_single_scalar(tmp_i[:, :], src_i[:, :], P - 1, ALU.bitwise_and))
            step(dve.tensor_copy(src_lo[:, :], tmp_i[:, :]))
            step(dve.tensor_single_scalar(tmp_i[:, :], src_i[:, :], 7, ALU.arith_shift_right))
            step(dve.tensor_copy(src_hi[:, :], tmp_i[:, :]))
            step(dve.memset(src_hi[0:REPEATED, (NB - 1) * J:], -1.0))
            dve.wait_ge(any_sum, 1)
            step(dve.tensor_copy(any_i[0:1, :], wide[1][0:1, 0:1]))
            dve.sem_inc(flag_ready, 1)
            dve.wait_ge(w_in, 32)

            near_blocks(GNN0, 0)
            read_sums(GNN0, NB)
            step(dve.tensor_tensor(tmp[:, :, :], x[:, :, :], agg[:, :, 0:F], ALU.add))
            layer_norm(tmp[:, :, :], x[:, :, :])
            dve.sem_inc(x_ready, 1)
            step(dve.tensor_scalar(stat[:, :], agg[:, :, F], 1.0, None, ALU.add))
            step(dve.tensor_scalar(stat2[:, :], stat[:, :], 0.0, None, ALU.is_gt))
            step(dve.tensor_scalar(dinv[:, :], stat[:, :], 1e-37, None, ALU.max))
            inverse_root(dinv)
            step(dve.tensor_tensor(dinv[:, :], dinv[:, :], stat2[:, :], ALU.mult))

            step(dve.memset(seed[:, :, F:W1], 1.0))
            for g in range(-(-NT // 4)):
                n = min(4, NT - 4 * g)
                dve.wait_ge(prod_done, NT + g + 1)
                dve.tensor_tensor(seed[:, 4 * g:4 * g + n, 0:F], wide[g % 2][:, 0:n * F].rearrange("p (t f) -> p t f", f=F),
                                  dinv[:, 4 * g:4 * g + n].unsqueeze(2).to_broadcast([P, n, F]), ALU.mult)\
                   .then_inc(prod_used, 1)
            dve.wait_ge(prod_used, 2 + NT + -(-NT // 4))
            dve.sem_inc(table_ready, 1)
            dve.sem_inc(seed_ready, 1)
            near_blocks(GNN1, NB)
            read_sums(GNN1, 2 * NB)
            step(dve.tensor_scalar(deg_out[:, :], degs, 1.0, None, ALU.add))
            step(dve.tensor_tensor(tmp[:, :, :], agg[:, :, 0:F], rowwise(dinv[:, :]), ALU.mult))
            step(dve.tensor_tensor(tmp[:, :, :], tmp[:, :, :], featurewise(g_bias[:, :]), ALU.add))
            layer_norm(tmp[:, :, :], agg[:, :, 0:F])
            step(dve.tensor_tensor(tmp[:, :, :], agg[:, :, 0:F], featurewise(gamma[:, :]), ALU.mult))
            step(dve.tensor_tensor(tmp[:, :, :], tmp[:, :, :], featurewise(beta[:, :]), ALU.add))
            dve.sem_inc(gelu_in, 1)
            dve.wait_ge(gelu_done, 1)
            step(dve.tensor_tensor(tmp[:, :, :], x[:, :, :], xc[:, :, :], ALU.add))
            layer_norm(tmp[:, :, :], x[:, :, :])

            dve.wait_ge(table_out, 32)
            step(dve.tensor_scalar(stat[:, :], deg_out[:, :], 1.0, None, ALU.max))
            inverse_root(stat)
            step(dve.tensor_tensor(seed[:, :, 0:F], x[:, :, :], rowwise(stat[:, :]), ALU.mult))
            dve.sem_inc(table_ready, 1)
            dve.sem_inc(seed_ready, 1)
            near_blocks(GNN2, 2 * NB)
            read_sums(GNN2, 3 * NB)
            step(dve.tensor_scalar(stat[:, :], agg[:, :, F], 1.0, None, ALU.max))
            inverse_root(stat)
            step(dve.tensor_tensor(tmp[:, :, :], agg[:, :, 0:F], rowwise(stat[:, :]), ALU.mult))
            step(dve.tensor_tensor(tmp[:, :, :], tmp[:, :, :], x[:, :, :], ALU.add))
            layer_norm(tmp[:, :, :], x[:, :, :])

            dve.sem_inc(table_ready, 1)
            dve.wait_ge(table_out, 64)
            step(dve.memset(seed[:, :, :], 0.0))
            dve.sem_inc(seed_ready, 1)
            read_sums(GNN3, 4 * NB)
            step(dve.tensor_scalar(stat[:, :], agg[:, :, F], 0.0, None, ALU.is_gt))
            step(dve.tensor_scalar(stat2[:, :], stat[:, :], -1.0, 1.0, ALU.mult, ALU.add))
            step(dve.tensor_tensor(stat[:, :], stat[:, :], agg[:, :, F], ALU.mult))
            step(dve.tensor_tensor(stat[:, :], stat[:, :], stat2[:, :], ALU.add))
            step(dve.reciprocal(stat[:, :], stat[:, :]))
            step(dve.tensor_tensor(tmp[:, :, :], agg[:, :, 0:F], rowwise(stat[:, :]), ALU.mult))
            step(dve.tensor_tensor(tmp[:, :, :], tmp[:, :, :], x[:, :, :], ALU.add))
            layer_norm(tmp[:, :, :], x[:, :, :])
            dve.sem_inc(table_ready, 1)


INPUTS = ["x", "src", "dst", "edge_attr_64", "edge_type_8", "edge_weight1", "L0_gnn_weight", "L0_gnn_h_bias",
          "L0_gnn_loop_weight", "L1_gnn_W", "L1_gnn_b", "L1_gnn_gamma", "L1_gnn_beta", "L3_gnn_W1", "L3_gnn_b1",
          "L3_gnn_W2", "L3_gnn_b2", "L3_gnn_linear_coef"]


def kernel(**inputs):
    import numpy as np
    import concourse.bacc as bacc
    from concourse.bass_utils import run_bass_kernel_spmd

    nc = bacc.Bacc("TRN2", target_bir_lowering=False, num_devices=1)
    arrays, A = {}, {}
    for name in INPUTS:
        a = np.ascontiguousarray(inputs[name])
        arrays["in_" + name] = a
        A[name] = nc.dram_tensor("in_" + name, a.shape, mybir.dt.from_np(a.dtype), kind="ExternalInput").ap()
    out = nc.dram_tensor("out_0", (N, F), F32, kind="ExternalOutput").ap()
    build(nc, A, out)
    result = run_bass_kernel_spmd(nc, [arrays], core_ids=[0])
    return result.results[0]["out_0"]
```

```python
import concourse.bass as bass
from concourse import mybir

N = 3125
F = 64
E = 103125
R = 8
P = 128
NT = -(-N // P)
TAIL = N - (NT - 1) * P
J = 15
BE = P * J
NB = -(-E // BE)
assert NB % 2 == 0
LAST = E - BE
REPEATED = ((NB - 1) * BE - LAST) // J
assert REPEATED * J == (NB - 1) * BE - LAST
WINDOW = 128
W1 = F + 1
BANK_TILES = [(0, 7), (7, 14), (14, 21), (21, NT)]
PAIRS = [(0, 1, 2), (3, 4, 5), (6, 7)]
TRIO = 3
TRIOS = J // TRIO
assert TRIOS % 2 == 1
SLOT_ROWS = NT + 1
EPS = 1e-5

F32 = mybir.dt.float32
BF16 = mybir.dt.bfloat16
I32 = mybir.dt.int32
ALU = mybir.AluOpType
ACT = mybir.ActivationFunctionType
AX = mybir.AxisListType.X
GNN0, GNN1, GNN2, GNN3 = range(4)


def build(nc, A, out):
    def sb(name, shape, dt=F32):
        return nc.alloc_sbuf_tensor(name, list(shape), dt)

    def sem(name):
        return nc.alloc_semaphore(name)

    table = [nc.dram_tensor("table_typed", (N * R, F), F32, kind="Internal").ap(),
             nc.dram_tensor("table_gcn", (N, F), F32, kind="Internal").ap(),
             nc.dram_tensor("table_sym", (N, F), F32, kind="Internal").ap(),
             nc.dram_tensor("table_attn", (N, F), F32, kind="Internal").ap()]
    table_parts = nc.dram_tensor("table_parts", (N, 3 * F), BF16, kind="Internal").ap()
    scattered = [[nc.dram_tensor(f"scattered{g}_{k}", (P * SLOT_ROWS, W1), F32, kind="Internal").ap()
                  for k in range(TRIO)] for g in range(2)]
    ends = nc.dram_tensor("ends", (4, NB, BE), BF16, kind="Internal").ap()

    iota_row = sb("iota_row", [P, P])
    iota_tile = sb("iota_tile", [P, NT])
    row_no = sb("row_no", [P, 1])
    ident = sb("ident", [P, P])
    ones = sb("ones", [P, P])
    zero_mat = sb("zero_mat", [P, P])

    src_i = sb("src_i", [P, NB * J], I32)
    dst_i = sb("dst_i", [P, NB * J], I32)
    type_i = sb("type_i", [P, NB * J], I32)
    typed_i = sb("typed_i", [P, NB * J], I32)
    weight = sb("weight", [P, NB * J])
    tmp_i = sb("tmp_i", [P, NB * J], I32)
    rel = sb("rel", [P, NB * J])
    src_lo = sb("src_lo", [P, NB * J])
    src_hi = sb("src_hi", [P, NB * J])
    far_lo = sb("far_lo", [P, NB * J])
    far_hi = sb("far_hi", [P, NB * J])
    outside = sb("outside", [P, NB * J])
    src_f = sb("src_f", [P, NB * J])
    earlier = sb("earlier", [P, NB * J])
    inside = earlier
    scat_i = sb("scat_i", [P, NB * J], I32)
    first_f = sb("first_f", [1, NB])
    first = sb("first", [P, NB])
    win_i = sb("win_i", [P, NB], I32)
    win_t = sb("win_t", [P, NB], I32)
    win_lo = sb("win_lo", [P, NB])
    win_hi = sb("win_hi", [P, NB])
    win_mask = sb("win_mask", [P, NB, NT])
    win_f = sb("win_f", [P, NB])
    win_row = sb("win_row", [P, NB], I32)
    any_col = sb("any_col", [P, 1])
    any_i = sb("any_i", [1, 1], I32)

    x = sb("x", [P, NT, F])
    xc = sb("xc", [P, NT, F])
    tmp = sb("tmp", [P, NT, F])
    agg = sb("agg", [P, NT, W1])
    seed = sb("seed", [P, NT, W1])
    stat = sb("stat", [P, NT])
    stat2 = sb("stat2", [P, NT])
    dinv = sb("dinv", [P, NT])
    deg_out = sb("deg_out", [P, NT])
    stage = sb("stage", [P, 2, R * F])

    w_types = sb("w_types", [F, R, F])
    w_loop = sb("w_loop", [F, W1])
    w_gcn = sb("w_gcn", [F, F])
    h_bias = sb("h_bias", [P, F])
    g_bias = sb("g_bias", [P, F])
    gamma = sb("gamma", [P, F])
    beta = sb("beta", [P, F])
    mlp1 = sb("mlp1", [P, P])
    mlp2 = sb("mlp2", [P, P])
    mlp_b1 = sb("mlp_b1", [P, 1])
    mlp_b2 = sb("mlp_b2", [P, F])
    coef = sb("coef", [P, F])

    idx = sb("idx", [P, 2, J], I32)
    rows = [sb(f"rows{s}", [P, J, W1]) for s in range(2)]
    msg = [sb(f"msg{s}", [P, J, W1]) for s in range(2)]
    hot = [sb(f"hot{s}", [P, J, P]) for s in range(2)]
    far_idx = sb("far_idx", [P, 2, J], I32)
    attn = sb("attn", [P, 2, J])
    weighted = sb("weighted", [P, J, W1])
    ends_row = [sb(f"ends_row{s}", [4, BE], BF16) for s in range(2)]
    take_src = sb("take_src", [4, P], BF16)
    take_dst = sb("take_dst", [4, P], BF16)
    before = sb("before", [P, P])
    win_x = [sb(f"win_x{s}", [P, 3 * F], BF16) for s in range(2)]
    win_idx = sb("win_idx", [P, 2], I32)
    whole = [h[:, :, :].rearrange("p j e -> p (j e)") for h in hot]
    ends_i, last_i = (whole[0][r, :].bitcast(I32) for r in (slice(0, NB - 1), slice(64, 65)))
    ends_f, last_f = ends_i.bitcast(F32), last_i.bitcast(F32)
    ends_a, last_a = (whole[1][r, 0:BE // 2].bitcast(BF16) for r in (slice(0, NB - 1), slice(64, 65)))
    ends_b, last_b = (whole[1][r, BE // 2:BE].bitcast(BF16) for r in (slice(0, NB - 1), slice(64, 65)))
    logit = sb("logit", [P, 2, J])
    prod = sb("prod", [P, J, F])
    mlp_out = [sb(f"mlp_out{s}", [P, J, F]) for s in range(2)]
    ea = [sb(f"ea{s}", [P, J * F]) for s in range(2)]
    eaT = [sb(f"eaT{u}", [P, 3 * P]) for u in range(3)]
    hidT = [sb(f"hidT{u}", [P, 3 * P]) for u in range(3)]
    spread = [sb(f"spread{s}", [P, SLOT_ROWS, W1]) for s in range(2)]
    spread_hot = sb("spread_hot", [P, 2, P])
    far_mask = sb("far_mask", [P, 2, NT])
    shared = sb("shared", [P, 2 * J * P])
    halves = [shared[:, s * J * P:(s + 1) * J * P] for s in range(2)]
    xT = shared[0:F, 0:NT * P]
    x_parts = shared[:, 0:NT * 3 * F // 2].bitcast(BF16).rearrange("p (t k f) -> p t k f", k=3, f=F)
    dst_hot = [halves[0][:, s * J * P // 2:(s + 1) * J * P // 2].bitcast(BF16).rearrange("p (j e) -> p j e", e=P)
               for s in range(2)]
    far_x = [halves[0][:, s * J * F:(s + 1) * J * F].rearrange("p (j f) -> p j f", f=F) for s in range(2)]
    parts = [a[:, 0:3 * J * W1 // 2 + 1].bitcast(BF16)[:, 0:3 * J * W1].rearrange("p (k j f) -> p k j f", k=3, f=W1)
             for a in (halves[1], seed[:, :, :].rearrange("p t f -> p (t f)"))]
    src_same = [h[:, 0:J * P // 2].bitcast(BF16).rearrange("p (j e) -> p j e", e=P) for h in whole]
    same = [h.rearrange("p (j e) -> p j e", e=P) for h in halves]
    src_hot = [shared[:, s * J * P // 2:(s + 1) * J * P // 2].bitcast(BF16).rearrange("p (j e) -> p j e", e=P)
               for s in range(2)]
    src_tile = [sb(f"src_tile{s}", [P, J, NT], BF16) for s in range(2)]

    sums = [nc.alloc_psum_tensor(f"sums{g}", [P, 512], F32) for g in range(4)]
    bank_t = nc.alloc_psum_tensor("bank_t", [P, 512], F32)
    bank_h = nc.alloc_psum_tensor("bank_h", [P, 512], F32)
    wide = [nc.alloc_psum_tensor(f"wide{g}", [P, 512], F32) for g in range(2)]
    part = [bank_t[:, 384:384 + W1], bank_h[:, 384:384 + W1]]
    degs = wide[0][:, 0:NT]

    src_in, dst_in, x_in, wts_in, w_in = sem("src_in"), sem("dst_in"), sem("x_in"), sem("wts_in"), sem("w_in")
    consts = sem("consts")
    zeroed = sem("zeroed")
    dve_step = sem("dve_step")
    pool_copied = sem("pool_copied")
    first_cast = sem("first_cast")
    first_bc = sem("first_bc")
    any_sum = sem("any_sum")
    any_col_ready = sem("any_col_ready")
    flag_ready = sem("flag_ready")
    prep_ready = sem("prep_ready")
    idx0_ready = sem("idx0_ready")
    x_ready = sem("x_ready")
    tr_done = sem("tr_done")
    tr_copied = sem("tr_copied")
    prod_done = sem("prod_done")
    prod_used = sem("prod_used")
    stage_out = [sem("stage_out0"), sem("stage_out1")]
    seed_ready = sem("seed_ready")
    table_ready = sem("table_ready")
    table_out = sem("table_out")
    out_done = sem("out_done")
    src_hot_ready = sem("src_hot_ready")
    src_hot_used = sem("src_hot_used")
    root_in, root_done = sem("root_in"), sem("root_done")
    gelu_in, gelu_done = sem("gelu_in"), sem("gelu_done")

    ends_loaded = sem("ends_loaded")
    ends_cast = sem("ends_cast")
    ends_out = sem("ends_out")
    cleared = sem("cleared")
    landed = [sem("landed0"), sem("landed1")]
    scatter_ready = sem("scatter_ready")
    pool_seen = sem("pool_seen")
    hi_ready, mid_ready = sem("hi_ready"), sem("mid_ready")
    rest_ready = sem("rest_ready")
    parts_ready = sem("parts_ready")
    parts_out = sem("parts_out")
    final_in = sem("final_in")

    class Sems:

        def __init__(self, way):
            self.rows_in = [sem(f"{way}_rows_in{s}") for s in range(2)]
            self.idx_staged = sem(f"{way}_idx_staged")
            self.ends_in = [sem(f"{way}_ends_in{s}") for s in range(2)]
            self.broadcast = sem(f"{way}_broadcast")
            self.compared = sem(f"{way}_compared")

    class SumSems(Sems):

        def __init__(self, way):
            super().__init__(way)
            self.main_done = sem(f"{way}_main_done")
            self.hot_ready = sem(f"{way}_hot_ready")
            self.spread_ready = sem(f"{way}_spread_ready")
            self.merged = sem(f"{way}_merged")
            self.mask_done = sem(f"{way}_mask_done")

    class AttendSems(Sems):

        def __init__(self, way):
            super().__init__(way)
            self.windowed = True
            self.win_in = [sem(f"{way}_win_in{s}") for s in range(2)]
            self.ea_in = [sem(f"{way}_ea_in{s}") for s in range(2)]
            self.taken = sem(f"{way}_taken")
            self.part_ready = sem(f"{way}_part_ready")
            self.part_cast = sem(f"{way}_part_cast")
            self.weighted = sem(f"{way}_weighted")
            self.seen = sem(f"{way}_seen")
            self.seen_copied = sem(f"{way}_seen_copied")
            self.blocks_in = sem(f"{way}_blocks_in")
            self.msg_done = sem(f"{way}_msg_done")
            self.prod_ready = sem(f"{way}_prod_ready")
            self.logit_ready = sem(f"{way}_logit_ready")
            self.attn_ready = sem(f"{way}_attn_ready")
            self.t_ready = sem(f"{way}_t_ready")
            self.t_copied = sem(f"{way}_t_copied")
            self.h_ready = sem(f"{way}_h_ready")
            self.hid_ready = sem(f"{way}_hid_ready")
            self.unit_done = sem(f"{way}_unit_done")
            self.mlp_copied = sem(f"{way}_mlp_copied")

    near, far, attend = SumSems("near"), SumSems("far"), AttendSems("attend")
    SLOTS = 2
    FAR_SLOTS = 2 * J

    def bank_of(banks, s, n, S):
        return banks[(s * casts_of(S) + n) % 2]

    def casts_of(S):
        return TRIOS if S is near or not S.windowed else 2 * TRIOS

    finals = [t[:, :, :] for t in spread]
    for big in (*whole, *halves):
        finals.append(big[:, 0:SLOT_ROWS * W1].rearrange("p (t f) -> p t f", f=W1))

    def edges(a):
        return a[0:(NB - 1) * BE].rearrange("(b p j) -> p b j", p=P, j=J)

    def blocks(eng, body, peel):
        if peel:
            with eng.Fori(0, NB // 2 - 1) as i:
                body(i, False)
            body(NB // 2 - 1, True)
        else:
            with eng.Fori(0, NB // 2) as i:
                body(i, False)

    def attend_way(eng, run):
        count = eng.value_load(any_i[0:1, 0:1], min_val=0, max_val=NB * BE)
        with eng.If(count > 0):
            attend.windowed = False
            run(attend)
        with eng.Else():
            attend.windowed = True
            run(attend)

    def far_way(eng, run):
        count = eng.value_load(any_i[0:1, 0:1], min_val=0, max_val=NB * BE)
        with eng.If(count > 0):
            run()

    with nc.Block() as block:

        @block.sync
        def _(sp):
            flat_w = A["edge_weight1"].rearrange("e o -> (e o)")
            for t, a, s in ((src_i, A["src"], src_in), (type_i, A["edge_type_8"], src_in),
                            (dst_i, A["dst"], dst_in)):
                sp.dma_start(t[:, 0:(NB - 1) * J].rearrange("p (b j) -> p b j", j=J), edges(a)).then_inc(s, 16)
                sp.dma_start(t[:, (NB - 1) * J:], a[LAST:E].rearrange("(p j) -> p j", j=J)).then_inc(s, 16)
            sp.dma_start(weight[:, 0:(NB - 1) * J].rearrange("p (b j) -> p b j", j=J), edges(flat_w))\
              .then_inc(w_in, 16)
            sp.dma_start(weight[:, (NB - 1) * J:], flat_w[LAST:E].rearrange("(p j) -> p j", j=J)).then_inc(w_in, 16)

            for r, name in ((0, "src"), (2, "dst")):
                if r:
                    sp.wait_ge(ends_cast, 8)
                sp.dma_start(ends_i[:, :], A[name][0:(NB - 1) * BE].rearrange("(b e) -> b e", e=BE)).then_inc(ends_loaded, 16)
                sp.dma_start(last_i[:, :], A[name][LAST:E].rearrange("(o e) -> o e", o=1)).then_inc(ends_loaded, 16)
                sp.wait_ge(ends_cast, 8 * (r // 2) + 8)
                for k, (most, last) in enumerate(((ends_a, last_a), (ends_b, last_b))):
                    sp.dma_start(ends[r + k, 0:NB - 1, :], most[:, :]).then_inc(ends_out, 16)
                    sp.dma_start(ends[r + k, NB - 1:NB, :], last[:, :]).then_inc(ends_out, 16)

            for t in range(NT):
                n = P if t < NT - 1 else TAIL
                sp.wait_ge(table_ready, t + 1)
                sp.dma_start(table[GNN0][t * P * R:(t * P + n) * R, :].rearrange("(p r) f -> p (r f)", r=R),
                             stage[0:n, t % 2, :]).then_inc(stage_out[t % 2], 16)

            sp.wait_ge(ends_out, 16 * 8)

            def ends_load(i, last):
                for s in range(2):
                    sp.wait_ge(near.broadcast, TRIOS * (2 * i + s) + TRIOS)
                    sp.dma_start(ends_row[s][:, :], ends[:, bass.ds(2 * i + s, 1), :].rearrange("r b e -> r (b e)"))\
                      .then_inc(near.ends_in[s], 16)
            blocks(sp, ends_load, False)

            for layer, source in ((GNN1, seed), (GNN2, seed), (GNN3, x)):
                sp.wait_ge(table_ready, NT + layer)
                sp.dma_start(table[layer][0:(NT - 1) * P, :].rearrange("(t p) f -> p t f", p=P),
                             source[:, 0:NT - 1, 0:F]).then_inc(table_out, 16)
                sp.dma_start(table[layer][(NT - 1) * P:N, :], source[0:TAIL, NT - 1, 0:F]).then_inc(table_out, 16)
            sp.wait_ge(parts_ready, 1)
            sp.dma_start(table_parts[0:(NT - 1) * P, :].rearrange("(t p) f -> p t f", p=P),
                         x_parts[:, 0:NT - 1, :, :].rearrange("p t k f -> p t (k f)")).then_inc(parts_out, 16)
            sp.dma_start(table_parts[(NT - 1) * P:N, :],
                         x_parts[0:TAIL, NT - 1, :, :].rearrange("p k f -> p (k f)")).then_inc(parts_out, 16)

            def attributes(S):
                def load(i, s, start):
                    sp.wait_ge(S.broadcast, casts_of(S) * (2 * i + s) + casts_of(S))
                    sp.dma_start(ends_row[s][:, :], ends[:, bass.ds(2 * i + s, 1), :].rearrange("r b e -> r (b e)"))\
                      .then_inc(S.ends_in[s], 16)
                    sp.wait_ge(S.unit_done, 3 * (2 * i + s) + 3)
                    sp.dma_start(ea[s][:, :], A["edge_attr_64"][bass.ds(start, BE), :]
                                 .rearrange("(p j) f -> p (j f)", j=J)).then_inc(S.ea_in[s], 16)

                def body(i, last):
                    load(i, 0, i * (2 * BE))
                    load(i, 1, LAST if last else i * (2 * BE) + BE)
                blocks(sp, body, True)

            sp.wait_ge(flag_ready, 1)
            attend_way(sp, attributes)
            for g in range(2):
                sp.wait_ge(landed[g], 16 * TRIO * (1 + NB * TRIOS // 2))
                for k in range(TRIO):
                    sp.dma_start(finals[g * TRIO + k].rearrange("p t f -> p (t f)"),
                                 scattered[g][k].rearrange("(p t) f -> p (t f)", p=P)).then_inc(final_in, 16)

            sp.wait_ge(table_ready, NT + 4)
            sp.dma_start(out[0:(NT - 1) * P, :].rearrange("(t p) f -> p t f", p=P), x[:, 0:NT - 1, :])\
              .then_inc(out_done, 16)
            sp.dma_start(out[(NT - 1) * P:N, :], x[0:TAIL, NT - 1, :]).then_inc(out_done, 16)
            sp.wait_ge(out_done, 32)

        @block.gpsimd
        def _(pool):
            pool.iota(iota_row[:, :], pattern=[[1, P]], base=0, channel_multiplier=0,
                      allow_small_or_imprecise_dtypes=True).then_inc(consts, 1)
            pool.iota(iota_tile[:, :], pattern=[[1, NT]], base=0, channel_multiplier=0,
                      allow_small_or_imprecise_dtypes=True).then_inc(consts, 1)
            pool.iota(row_no[:, :], pattern=[[0, 1]], base=0, channel_multiplier=1,
                      allow_small_or_imprecise_dtypes=True).then_inc(consts, 1)

            def gathers(layer, S, v0):
                index = typed_i if layer == GNN0 else src_i

                def body(i, last):
                    for s in range(2):
                        v = 2 * i + s
                        if S is near:
                            pool.wait_ge(S.main_done, v0 + v + 1)
                        else:
                            pool.wait_ge(S.merged, (v0 + v) * J + J)
                        pool.tensor_copy(idx[:, s, :], index[:, bass.ds(v * J, J)]).then_inc(S.idx_staged, 1)
                        pool.wait_ge(S.idx_staged, 1)
                        pool.sem_clear(S.idx_staged)
                        for j in range(J):
                            pool.indirect_dma_start(
                                out=rows[s][:, j, 0:F], out_offset=None, in_=table[layer][:, :],
                                in_offset=bass.IndirectOffsetOnAxis(ap=idx[:, s, j:j + 1], axis=0),
                            ).then_inc(S.rows_in[s], 16)
                blocks(pool, body, False)

            pool.wait_ge(consts, 3)
            for n in range(2):
                pool.wait_ge(ends_loaded, 32 * (n + 1))
                if n:
                    pool.wait_ge(ends_out, 16 * 4)
                at = 8 * n
                for i_, f_, a_, b_ in ((ends_i, ends_f, ends_a, ends_b), (last_i, last_f, last_a, last_b)):
                    pool.tensor_copy(f_[:, :], i_[:, :]).then_inc(ends_cast, 1)
                    pool.wait_ge(ends_cast, at + 1)
                    pool.tensor_copy(a_[:, :], f_[:, :]).then_inc(ends_cast, 1)
                    pool.wait_ge(ends_cast, at + 2)
                    pool.tensor_tensor(b_[:, :], f_[:, :], a_[:, :], ALU.subtract).then_inc(ends_cast, 1)
                    pool.wait_ge(ends_cast, at + 3)
                    at += 3
                pool.memset(last_a[:, 0:REPEATED * J], -1.0).then_inc(ends_cast, 1)
                pool.wait_ge(ends_cast, at + 1)
                pool.memset(last_b[:, 0:REPEATED * J], 0.0).then_inc(ends_cast, 1)
                pool.wait_ge(ends_cast, at + 2)
            pool.wait_ge(cleared, 1)
            for g in range(2):
                for k in range(TRIO):
                    pool.dma_start(scattered[g][k].rearrange("(p t) f -> p (t f)", p=P),
                                   spread[0][:, :, :].rearrange("p t f -> p (t f)")).then_inc(landed[g], 16)
            pool.wait_ge(idx0_ready, 1)
            for layer in range(3):
                if layer == GNN0:
                    pool.wait_ge(stage_out[0], 16 * ((NT + 1) // 2))
                    pool.wait_ge(stage_out[1], 16 * (NT // 2))
                else:
                    pool.wait_ge(table_out, 32 * layer)
                gathers(layer, near, layer * NB)
                if layer == GNN0:
                    pool.wait_ge(flag_ready, 1)
                pool.wait_ge(near.main_done, SLOTS + (layer + 1) * NB)
                far_way(pool, lambda: gathers(layer, far, layer * NB))

            def scatters(S):
                def fetch(i, s, v):
                    if S.windowed:
                        pool.tensor_copy(win_idx[:, s:s + 1], win_row[:, bass.ds(v, 1)]).then_inc(S.idx_staged, 1)
                    else:
                        pool.tensor_copy(far_idx[:, s, :], dst_i[:, bass.ds(v * J, J)]).then_inc(S.idx_staged, 1)
                    pool.wait_ge(S.idx_staged, 1)
                    pool.sem_clear(S.idx_staged)
                    if S.windowed:
                        pool.indirect_dma_start(
                            out=win_x[s][:, :], out_offset=None, in_=table_parts[:, :],
                            in_offset=bass.IndirectOffsetOnAxis(ap=win_idx[:, s:s + 1], axis=0)).then_inc(S.win_in[s], 16)
                        return
                    for j in range(J):
                        pool.indirect_dma_start(
                            out=far_x[s][:, j, :], out_offset=None, in_=table[GNN3][:, :],
                            in_offset=bass.IndirectOffsetOnAxis(ap=far_idx[:, s, j:j + 1], axis=0)).then_inc(S.rows_in[s], 16)

                def body(i, last):
                    for s in range(2):
                        v = 2 * i + s
                        pool.tensor_copy(idx[:, s, :], scat_i[:, bass.ds(v * J, J)]).then_inc(S.idx_staged, 1)
                        pool.wait_ge(S.idx_staged, 1)
                        pool.sem_clear(S.idx_staged)
                        for q in range(TRIOS):
                            n = s * TRIOS + q
                            pool.wait_ge(S.seen_copied, v * TRIOS + q + 1 + SLOTS)
                            pool.sem_inc(pool_seen, 1)
                            if q == 0 and not (last and s == 1):
                                fetch(i, 1 - s, v + 1)
                            pool.wait_ge(landed[n % 2], i * (16 * TRIO * TRIOS) + 16 * TRIO * (n // 2 + 1))
                            pool.sem_inc(pool_seen, 1)
                            if q == 1:
                                pool.sem_inc(S.blocks_in, 1)
                            for k in range(TRIO):
                                j = q * TRIO + k
                                pool.indirect_dma_start(
                                    out=scattered[n % 2][k][:, :],
                                    out_offset=bass.IndirectOffsetOnAxis(ap=idx[:, s, j:j + 1], axis=0),
                                    in_=rows[s][:, j, :], in_offset=None, compute_op=ALU.add).then_inc(landed[n % 2], 16)
                pool.sem_inc(S.blocks_in, 1)
                fetch(0, 0, 0)
                blocks(pool, body, True)

            pool.wait_ge(scatter_ready, 1)
            pool.wait_ge(table_out, 32 * GNN3)
            pool.wait_ge(parts_out, 32)
            attend_way(pool, scatters)

        @block.scalar
        def _(act):
            act.dma_start(x[:, 0:NT - 1, :], A["x"][0:(NT - 1) * P, :].rearrange("(t p) f -> p t f", p=P))\
               .then_inc(x_in, 16)
            act.wait_ge(zeroed, 1)
            act.dma_start(x[0:TAIL, NT - 1, :], A["x"][(NT - 1) * P:N, :]).then_inc(x_in, 16)
            act.dma_start(w_types[:, :, :], A["L0_gnn_weight"].rearrange("r i o -> i r o")).then_inc(wts_in, 16)
            act.dma_start(w_loop[:, 0:F], A["L0_gnn_loop_weight"]).then_inc(wts_in, 16)
            act.dma_start(w_gcn[:, :], A["L1_gnn_W"]).then_inc(wts_in, 16)
            for t, name in ((h_bias, "L0_gnn_h_bias"), (g_bias, "L1_gnn_b"), (gamma, "L1_gnn_gamma"),
                            (beta, "L1_gnn_beta"), (mlp_b2, "L3_gnn_b2")):
                act.dma_start(t[:, :], A[name].partition_broadcast(P)).then_inc(wts_in, 16)
            act.dma_start(coef[:, :], A["L3_gnn_linear_coef"].rearrange("f o -> (f o)").partition_broadcast(P))\
               .then_inc(wts_in, 16)
            for h in range(2):
                q = slice(h * F, (h + 1) * F)
                act.dma_start(mlp1[q, q], A["L3_gnn_W1"]).then_inc(wts_in, 16)
                act.dma_start(mlp2[q, q], A["L3_gnn_W2"]).then_inc(wts_in, 16)
                act.dma_start(mlp_b1[q, :], A["L3_gnn_b1"].rearrange("(f o) -> f o", o=1)).then_inc(wts_in, 16)

            def copy_transposed(base):
                for g in range(-(-NT // 4)):
                    n = min(4, NT - 4 * g) * P
                    act.wait_ge(tr_done, base + g + 1)
                    act.activation(xT[:, 4 * g * P:4 * g * P + n], (bank_t, bank_h)[g % 2][0:F, 0:n], ACT.Copy)\
                       .then_inc(tr_copied, 1)

            roots = [0]

            def root(a):
                roots[0] += 1
                act.wait_ge(root_in, roots[0])
                act.activation(a[:, :], a[:, :], ACT.Sqrt).then_inc(root_done, 1)

            copy_transposed(0)
            root(stat2)
            copy_transposed(-(-NT // 4))
            root(dinv)
            root(stat2)
            act.wait_ge(gelu_in, 1)
            act.activation(xc[:, :, :], tmp[:, :, :], ACT.Gelu).then_inc(gelu_done, 1)
            root(stat2)
            root(stat)
            root(stat)
            root(stat2)

            def mlp(S):
                def transposed(v, u):
                    n = len(PAIRS[u]) * P
                    act.wait_ge(S.t_ready, 3 * v + u + 1)
                    act.activation(eaT[u][:, 0:n], bank_t[:, 0:n], ACT.Copy).then_inc(S.t_copied, 1)

                def hidden(v, u):
                    n = len(PAIRS[u]) * P
                    act.wait_ge(S.h_ready, 3 * v + u + 1)
                    act.wait_ge(S.unit_done, 3 * v + u + 4)
                    act.activation(hidT[u][:, 0:n], bank_h[:, 0:n], ACT.Tanh, bias=mlp_b1[:, 0:1])\
                       .then_inc(S.hid_ready, 1)

                def body(i, last):
                    for s in range(2):
                        v = 2 * i + s
                        ahead = not (last and s == 1)
                        if ahead:
                            transposed(v + 1, 0)
                            hidden(v + 1, 0)
                            transposed(v + 1, 1)
                        act.wait_ge(S.logit_ready, v + 1)
                        act.activation(attn[:, s, :], logit[:, s, :], ACT.Exp).then_inc(S.attn_ready, 1)
                        if ahead:
                            hidden(v + 1, 1)
                            transposed(v + 1, 2)
                        for k in range(2):
                            act.wait_ge(S.part_ready, 2 * v + k + 1)
                            act.activation(parts[s][:, k, :, :], weighted[:, :, :], ACT.Copy).then_inc(S.part_cast, 1)
                        if ahead:
                            hidden(v + 1, 2)
                        act.wait_ge(S.blocks_in, v + 1)
                        for q in range(TRIOS):
                            act.wait_ge(S.seen, v * TRIOS + q + 1)
                            act.activation(rows[s][:, q * TRIO:(q + 1) * TRIO, :],
                                           sums[2 + (s + q) % 2][:, 0:TRIO * W1].rearrange("p (j f) -> p j f", f=W1),
                                           ACT.Copy).then_inc(S.seen_copied, 1)
                for u in range(len(PAIRS)):
                    transposed(0, u)
                    hidden(0, u)
                blocks(act, body, True)

            act.wait_ge(table_ready, NT + GNN3)
            act.activation(x_parts[:, :, 0, :], x[:, :, :], ACT.Copy).then_inc(hi_ready, 1)
            act.wait_ge(rest_ready, 1)
            act.activation(x_parts[:, :, 1, :], tmp[:, :, :], ACT.Copy).then_inc(mid_ready, 1)
            act.wait_ge(wts_in, 16 * 15)
            act.wait_ge(flag_ready, 1)
            attend_way(act, mlp)
            root(stat2)

        @block.tensor
        def _(pe):
            pe.sem_inc(near.main_done, SLOTS)
            pe.sem_inc(near.merged, SLOTS)
            pe.sem_inc(far.merged, FAR_SLOTS)
            pe.sem_inc(src_hot_used, SLOTS)
            pe.sem_inc(attend.unit_done, SLOTS * len(PAIRS))
            pe.sem_inc(near.broadcast, SLOTS * TRIOS)

            def transpose_nodes(base):
                for g in range(-(-NT // 4)):
                    if g >= 2:
                        pe.wait_ge(tr_copied, base + g - 1)
                    for k in range(min(4, NT - 4 * g)):
                        last = pe.transpose((bank_t, bank_h)[g % 2][0:F, k * P:(k + 1) * P], x[:, 4 * g + k, :], ident[:, :])
                    last.then_inc(tr_done, 1)

            def start_sums(lhsT):
                for g, (t0, t1) in enumerate(BANK_TILES):
                    for t in range(t0, t1):
                        lhs, rhs = lhsT(t)
                        pe.matmul(sums[g][:, (t - t0) * W1:(t - t0 + 1) * W1], lhs, rhs,
                                  start=(t == t0), stop=True, skip_group_check=True)

            def merge(slot, done):
                for g, (t0, t1) in enumerate(BANK_TILES):
                    last = pe.matmul(sums[g][:, 0:(t1 - t0) * W1], spread_hot[:, slot, :],
                                     spread[slot][:, t0:t1, :].rearrange("p t f -> p (t f)"),
                                     start=False, stop=True, skip_group_check=True)
                last.then_inc(done, 1)

            def unit_transpose(S, v, k, s, u):
                if u == 0:
                    pe.wait_ge(S.ea_in[s], 16 * (k + 1))
                pe.wait_ge(S.t_copied, 3 * v + u + 1)
                for c, q in enumerate(PAIRS[u]):
                    at = min(2 * q, J - 2) * F
                    last = pe.transpose(bank_t[:, c * P:(c + 1) * P], ea[s][:, at:at + P], ident[:, :])
                last.then_inc(S.t_ready, 1)

            def unit_hidden(S, v, u, first=False):
                n = len(PAIRS[u]) * P
                pe.wait_ge(S.t_copied, 3 * v + u + 2)
                if not first:
                    pe.wait_ge(S.hid_ready, 3 * v + u)
                pe.matmul(bank_h[:, 0:n], mlp1[:, :], eaT[u][:, 0:n], start=True, stop=True)\
                  .then_inc(S.h_ready, 1)

            def unit_out(S, v, u):
                pe.wait_ge(S.hid_ready, 3 * v + u + 1)
                if u == 0:
                    pe.wait_ge(S.mlp_copied, v + 1)
                for c, q in enumerate(PAIRS[u]):
                    at = min(2 * q, J - 2) * F
                    last = pe.matmul(wide[at // 512][:, at % 512:at % 512 + P], hidT[u][:, c * P:(c + 1) * P],
                                     mlp2[:, :], start=True, stop=True)
                last.then_inc(S.unit_done, 1)

            def broadcast(S, v, k, s, n, take, banks):
                if n == 0:
                    pe.wait_ge(S.ends_in[s], 16 * (k + 1))
                pe.wait_ge(S.compared, casts_of(S) * v + n + 1)
                q = n % TRIOS
                chunks = ends_row[s][:, :].rearrange("r (p j) -> r j p", j=J)[:, q * TRIO:(q + 1) * TRIO, :]
                pe.matmul(bank_of(banks, s, n, S)[:, 0:TRIO * P], take[:, :], chunks, start=True, stop=True)\
                  .then_inc(S.broadcast, 1)

            def near_blocks(layer, v0):
                S = near

                def body(i, last):
                    for s in range(2):
                        v = 2 * i + s
                        if layer == GNN1:
                            pe.wait_ge(src_hot_ready, v + 1)
                            for j in range(J):
                                mm = pe.matmul(degs, src_hot[s][:, j, :], src_tile[s][:, j, :],
                                               start=False, stop=True, skip_group_check=True)
                            mm.then_inc(src_hot_used, 1)
                        pe.wait_ge(S.hot_ready, v0 + v + 1)
                        pe.wait_ge(S.rows_in[s], (i + v0 // 2) * (16 * J) + 16 * J)
                        for j in range(J):
                            mm = pe.matmul(part[s], hot[s][:, j, :], rows[s][:, j, :], start=(j == 0), stop=(j == J - 1))
                        mm.then_inc(S.main_done, 1)
                        if layer == GNN0:
                            for n in (0, 1):
                                broadcast(S, v, i, s, n, take_src, wide)
                        pe.wait_ge(S.spread_ready, v0 + v + 1)
                        merge(s, S.merged)
                        if layer == GNN0:
                            for n in range(2, TRIOS):
                                broadcast(S, v, i, s, n, take_src, wide)
                blocks(pe, body, False)

            def far_blocks(v0):
                def body(i, last):
                    for s in range(2):
                        for j in range(J):
                            pe.wait_ge(far.spread_ready, (v0 + 2 * i + s) * J + j + 1)
                            merge((s + j) % 2, far.merged)
                blocks(pe, body, False)

            def attend_blocks(S):
                of_dst = casts_of(S) - TRIOS

                def cast(v, k, s, n):
                    if n == of_dst:
                        pe.wait_ge(S.seen_copied, v * TRIOS + SLOTS)
                    broadcast(S, v, k, s, n, take_dst if n < of_dst else take_src, sums[2:4])

                def take(v, k, s, q):
                    if not S.windowed:
                        return
                    if q == 0:
                        pe.wait_ge(S.win_in[s], 16 * (k + 1))
                        pe.wait_ge(S.msg_done, v + 1)
                    pe.wait_ge(S.compared, casts_of(S) * v + q + 1 + SLOTS)
                    for j in range(q * TRIO, (q + 1) * TRIO):
                        for p in range(3):
                            mm = pe.matmul(sums[j // 8][:, j % 8 * F:j % 8 * F + F], dst_hot[s][:, j, :],
                                           win_x[s][:, p * F:(p + 1) * F], start=(p == 0), stop=(p == 2))
                    if q == TRIOS - 1:
                        mm.then_inc(S.taken, 1)

                def sum_same(v, s, after):
                    pe.wait_ge(S.weighted, v + 1)
                    pe.wait_ge(S.compared, after + SLOTS)
                    for q in range(TRIOS):
                        pe.wait_ge(S.seen_copied, v * TRIOS + q + 1)
                        for k in range(TRIO):
                            j = q * TRIO + k
                            for p in range(3):
                                mm = pe.matmul(sums[2 + (s + q) % 2][:, k * W1:(k + 1) * W1], src_same[s][:, j, :],
                                               parts[s][:, p, j, :], start=(p == 0), stop=(p == 2))
                        mm.then_inc(S.seen, 1)

                def body(i, last):
                    for s in range(2):
                        v = 2 * i + s
                        if last and s == 1:
                            sum_same(v, s, casts_of(S) * NB)
                            continue
                        w, k, t = v + 1, i + s, 1 - s
                        for u, n in ((0, range(0, 2)), (1, range(2, 3)), (2, range(3, 4))):
                            unit_transpose(S, w, k, t, u)
                            for c in n:
                                if c < of_dst:
                                    cast(w, k, t, c)
                            if u:
                                unit_out(S, w, u - 1)
                            if u < 2:
                                unit_hidden(S, w, u)
                        if of_dst:
                            cast(w, k, t, 4)
                        unit_hidden(S, w, 2)
                        sum_same(v, s, casts_of(S) * w + of_dst)
                        unit_out(S, w, 2)
                        for q in range(TRIOS):
                            cast(w, k, t, of_dst + q)
                            take(w, k, t, q)

                pe.sem_inc(S.broadcast, SLOTS * casts_of(S))
                for u in range(len(PAIRS)):
                    unit_transpose(S, 0, 0, 0, u)
                    unit_hidden(S, 0, u, first=(u == 0))
                    unit_out(S, 0, u)
                for n in range(casts_of(S)):
                    broadcast(S, 0, 0, 0, n, take_dst if n < of_dst else take_src, sums[2:4])
                for q in range(TRIOS):
                    take(0, 0, 0, q)
                blocks(pe, body, True)

            pe.wait_ge(x_ready, 1)
            transpose_nodes(0)
            pe.wait_ge(wts_in, 16 * 15)
            pe.wait_ge(tr_copied, -(-NT // 4))
            for t in range(NT):
                pe.wait_ge(prod_used, t + 1)
                pe.matmul(wide[t % 2][:, :], xT[:, t * P:(t + 1) * P], w_types[:, :, :].rearrange("i r o -> i (r o)"),
                          start=True, stop=True).then_inc(prod_done, 1)
            start_sums(lambda t: (xT[:, t * P:(t + 1) * P], w_loop[:, :]))
            pe.wait_ge(first_cast, 1)
            pe.matmul(wide[0][:, 0:NB], ones[0:1, :], first_f[0:1, :], start=True, stop=True).then_inc(first_bc, 1)
            pe.wait_ge(any_col_ready, 1)
            pe.matmul(wide[1][0:1, 0:1], any_col[:, 0:1], ones[:, 0:1], start=True, stop=True).then_inc(any_sum, 1)

            pe.wait_ge(flag_ready, 1)
            near_blocks(GNN0, 0)
            far_way(pe, lambda: far_blocks(0))

            pe.wait_ge(x_ready, 2)
            transpose_nodes(-(-NT // 4))
            pe.wait_ge(tr_copied, 2 * -(-NT // 4))
            for g in range(-(-NT // 4)):
                pe.wait_ge(prod_used, NT + g + 1)
                for k in range(min(4, NT - 4 * g)):
                    t = 4 * g + k
                    mm = pe.matmul(wide[g % 2][:, k * F:(k + 1) * F], xT[:, t * P:(t + 1) * P], w_gcn[:, :],
                                   start=True, stop=True)
                mm.then_inc(prod_done, 1)
            pe.wait_ge(seed_ready, 1)
            pe.matmul(degs, zero_mat[:, :], iota_tile[:, :], start=True, stop=True, skip_group_check=True)
            start_sums(lambda t: (ident[:, :], seed[:, t, :]))
            near_blocks(GNN1, NB)
            far_way(pe, lambda: far_blocks(NB))

            pe.wait_ge(seed_ready, 2)
            start_sums(lambda t: (ident[:, :], seed[:, t, :]))
            near_blocks(GNN2, 2 * NB)
            far_way(pe, lambda: far_blocks(2 * NB))

            pe.wait_ge(seed_ready, 3)
            attend_way(pe, attend_blocks)

        @block.vector
        def _(dve):
            steps = [0]

            def step(ins):
                steps[0] += 1
                ins.then_inc(dve_step, 1)
                dve.wait_ge(dve_step, steps[0])

            def rowwise(a):
                return a.unsqueeze(2).to_broadcast([P, NT, F])

            def featurewise(a):
                return a.unsqueeze(1).to_broadcast([P, NT, F])

            roots = [0]

            def inverse_root(a):
                roots[0] += 1
                step(dve.reciprocal(a[:, :], a[:, :]))
                dve.sem_inc(root_in, 1)
                dve.wait_ge(root_done, roots[0])

            def layer_norm(src, dst, mean=stat, var=stat2):
                step(dve.tensor_reduce(mean[:, :], src, axis=AX, op=ALU.add))
                step(dve.tensor_scalar(mean[:, :], mean[:, :], 1.0 / F, None, ALU.mult))
                step(dve.tensor_tensor(xc[:, :, :], src, rowwise(mean[:, :]), ALU.subtract))
                step(dve.tensor_tensor(dst, xc[:, :, :], xc[:, :, :], ALU.mult))
                step(dve.tensor_reduce(var[:, :], dst, axis=AX, op=ALU.add))
                step(dve.tensor_scalar(var[:, :], var[:, :], 1.0 / F, EPS, ALU.mult, ALU.add))
                inverse_root(var)
                step(dve.tensor_tensor(dst, xc[:, :, :], rowwise(var[:, :]), ALU.mult))

            def read_sums(layer, all_near):
                dve.wait_ge(near.merged, SLOTS + all_near)
                far_way(dve, lambda: far_blocks(layer, layer * NB))
                for g, (t0, t1) in enumerate(BANK_TILES):
                    last = dve.tensor_copy(agg[:, t0:t1, :], sums[g][:, 0:(t1 - t0) * W1].rearrange("p (t f) -> p t f", f=W1))
                step(last)

            def edge_scale(layer, s, j, c):
                return weight[:, bass.ds(c, 1)] if layer in (GNN0, GNN1) else None

            def one_hot(out_, numbers, value, scale):
                if scale is None:
                    return dve.tensor_scalar(out_, numbers, value, None, ALU.is_equal)
                return dve.tensor_scalar(out_, numbers, value, scale, ALU.is_equal, ALU.mult)

            def compare_src(S, v, s, n, banks):
                q = n % TRIOS
                dve.wait_ge(S.broadcast, casts_of(S) * (v + SLOTS) + n + 1)
                dve.tensor_tensor(src_same[s][:, q * TRIO:(q + 1) * TRIO, :],
                                  bank_of(banks, s, n, S)[:, 0:TRIO * P].rearrange("p (j e) -> p j e", e=P),
                                  src_f[:, bass.ds(v * J + q * TRIO, TRIO)].unsqueeze(2).to_broadcast([P, TRIO, P]),
                                  ALU.is_equal).then_inc(S.compared, 1)

            def compare_dst(S, v, s, n, banks):
                dve.wait_ge(S.broadcast, casts_of(S) * (v + SLOTS) + n + 1)
                dve.tensor_scalar(dst_hot[s][:, n * TRIO:(n + 1) * TRIO, :].rearrange("p j e -> p (j e)"),
                                  bank_of(banks, s, n, S)[:, 0:TRIO * P], win_f[:, bass.ds(v, 1)], None,
                                  ALU.is_equal).then_inc(S.compared, 1)

            def attend_blocks(S):
                of_dst = casts_of(S) - TRIOS

                def embeddings(v, s):
                    dve.wait_ge(S.unit_done, 3 * v + 9)
                    for g in range(2):
                        n = 8 if g == 0 else J - 8
                        mm = dve.tensor_tensor(mlp_out[s][:, 8 * g:8 * g + n, :],
                                               wide[g][:, 0:n * F].rearrange("p (j f) -> p j f", f=F),
                                               mlp_b2[:, :].unsqueeze(1).to_broadcast([P, n, F]), ALU.add)
                    mm.then_inc(S.mlp_copied, 1)

                def compare(v, s, n):
                    (compare_dst if n < of_dst else compare_src)(S, v, s, n, sums[2:4])

                def body(i, last):
                    for s in range(2):
                        v = 2 * i + s
                        w, t = v + 1, 1 - s
                        dsts = [] if last and s == 1 else list(range(of_dst))
                        dve.wait_ge(S.mlp_copied, v + 2)
                        dve.wait_ge(S.seen_copied, v * TRIOS + SLOTS)
                        if S.windowed:
                            dve.wait_ge(S.taken, v + 1)
                            for g in range(2):
                                n = 8 if g == 0 else J - 8
                                mm = dve.tensor_tensor(msg[s][:, 8 * g:8 * g + n, 0:F], mlp_out[s][:, 8 * g:8 * g + n, :],
                                                       sums[g][:, 0:n * F].rearrange("p (j f) -> p j f", f=F), ALU.mult)
                        else:
                            dve.wait_ge(S.rows_in[s], (i + 1) * (16 * J))
                            mm = dve.tensor_tensor(msg[s][:, :, 0:F], mlp_out[s][:, :, :], far_x[s], ALU.mult)
                        mm.then_inc(S.msg_done, 1)
                        dve.wait_ge(S.msg_done, v + 2)
                        dve.tensor_tensor(prod[:, :, :], msg[s][:, :, 0:F],
                                          coef[:, :].unsqueeze(1).to_broadcast([P, J, F]), ALU.mult).then_inc(S.prod_ready, 1)
                        dve.wait_ge(S.prod_ready, v + 1)
                        dve.tensor_reduce(logit[:, s, :], prod[:, :, :], axis=AX, op=ALU.add).then_inc(S.logit_ready, 1)
                        for n in dsts[0:2]:
                            compare(w, t, n)
                        dve.wait_ge(S.attn_ready, v + 1)
                        dve.tensor_tensor(weighted[:, :, :], msg[s][:, :, :],
                                          attn[:, s, :].unsqueeze(2).to_broadcast([P, J, W1]), ALU.mult).then_inc(S.part_ready, 1)
                        for n in dsts[2:3]:
                            compare(w, t, n)
                        dve.wait_ge(S.part_ready, 2 * v + 1)
                        dve.wait_ge(S.part_cast, 2 * v + 1)
                        dve.tensor_tensor(weighted[:, :, :], weighted[:, :, :], parts[s][:, 0, :, :], ALU.subtract)\
                           .then_inc(S.part_ready, 1)
                        for n in dsts[3:4]:
                            compare(w, t, n)
                        dve.wait_ge(S.part_ready, 2 * v + 2)
                        dve.wait_ge(S.part_cast, 2 * v + 2)
                        dve.tensor_tensor(parts[s][:, 2, :, :], weighted[:, :, :], parts[s][:, 1, :, :], ALU.subtract)\
                           .then_inc(S.weighted, 1)
                        for n in dsts[4:]:
                            compare(w, t, n)
                        if not (last and s == 1):
                            for n in range(of_dst, casts_of(S)):
                                compare(w, t, n)
                            embeddings(w, t)

                for n in range(casts_of(S)):
                    compare(0, 0, n)
                embeddings(0, 0)
                blocks(dve, body, True)

            def near_blocks(layer, v0):
                S = near

                def one_hots(v, s):
                    dve.wait_ge(S.main_done, v0 + v + 1)
                    for j in range(J):
                        mm = one_hot(hot[s][:, j, :], iota_row[:, :], rel[:, bass.ds(v * J + j, 1)],
                                     edge_scale(layer, s, j, v * J + j))
                    mm.then_inc(S.hot_ready, 1)

                def body(i, last):
                    for s in range(2):
                        v = 2 * i + s
                        if layer == GNN1:
                            dve.wait_ge(src_hot_used, v + 1)
                            dve.tensor_tensor(src_hot[s][:, :, :], iota_row[:, :].unsqueeze(1).to_broadcast([P, J, P]),
                                              src_lo[:, bass.ds(v * J, J)].unsqueeze(2).to_broadcast([P, J, P]), ALU.is_equal)
                            dve.tensor_tensor(src_tile[s][:, :, :], iota_tile[:, :].unsqueeze(1).to_broadcast([P, J, NT]),
                                              src_hi[:, bass.ds(v * J, J)].unsqueeze(2).to_broadcast([P, J, NT]), ALU.is_equal)\
                               .then_inc(src_hot_ready, 1)
                        if not (last and s == 1):
                            one_hots(v + 1, 1 - s)
                        dve.wait_ge(S.merged, v0 + v + 1)
                        one_hot(spread_hot[:, s, :], iota_row[:, :], win_lo[:, bass.ds(v, 1)], None)
                        dve.wait_ge(S.main_done, v0 + v + SLOTS + 1)
                        dve.tensor_tensor(spread[s][:, 0:NT, :], part[s].unsqueeze(1).to_broadcast([P, NT, W1]),
                                          win_mask[:, bass.ds(v, 1), :].rearrange("p b t -> p (b t)").unsqueeze(2)
                                          .to_broadcast([P, NT, W1]), ALU.mult).then_inc(S.spread_ready, 1)
                        if layer == GNN0:
                            for n in range(TRIOS):
                                dve.wait_ge(S.broadcast, TRIOS * (v + SLOTS) + n + 1)
                                for k in range(TRIO):
                                    c = v * J + n * TRIO + k
                                    mm = dve.scalar_tensor_tensor(
                                        same[s][:, n * TRIO + k, :], bank_of(wide, s, n, S)[:, k * P:(k + 1) * P], src_f[:, bass.ds(c, 1)],
                                        before[:, :], ALU.is_equal, ALU.mult, accum_out=earlier[:, bass.ds(c, 1)])
                                mm.then_inc(S.compared, 1)
                one_hots(0, 0)
                blocks(dve, body, True)

            def far_blocks(layer, v0):
                S = far

                def body(i, last):
                    for s in range(2):
                        v = 2 * i + s
                        dve.wait_ge(S.rows_in[s], (i + v0 // 2) * (16 * J) + 16 * J)
                        for j in range(J):
                            q = (s + j) % 2
                            g = (v0 + v) * J + j
                            dve.wait_ge(S.merged, g + FAR_SLOTS - 1)
                            dve.tensor_scalar(far_mask[:, q, :], iota_tile[:, :], far_hi[:, bass.ds(v * J + j, 1)],
                                              None, ALU.is_equal).then_inc(S.mask_done, 1)
                            one_hot(spread_hot[:, q, :], iota_row[:, :], far_lo[:, bass.ds(v * J + j, 1)],
                                    edge_scale(layer, s, j, v * J + j))
                            dve.wait_ge(S.mask_done, g + 1)
                            dve.tensor_tensor(spread[q][:, 0:NT, :],
                                              rows[s][:, j, :].unsqueeze(1).to_broadcast([P, NT, W1]),
                                              far_mask[:, q, :].unsqueeze(2).to_broadcast([P, NT, W1]), ALU.mult)\
                               .then_inc(S.spread_ready, 1)
                blocks(dve, body, False)
                dve.wait_ge(S.merged, FAR_SLOTS + (v0 + NB) * J)

            dve.sem_inc(attend.msg_done, 1)
            dve.sem_inc(attend.mlp_copied, 1)
            dve.sem_inc(attend.t_copied, 1)
            dve.sem_inc(attend.seen_copied, SLOTS)
            for S in (near, attend):
                dve.sem_inc(S.compared, SLOTS)
            dve.sem_inc(prod_used, 2)
            dve.memset(x[:, NT - 1, :], 0.0)
            dve.memset(mlp1[:, :], 0.0)
            dve.memset(mlp2[:, :], 0.0).then_inc(zeroed, 1)
            dve.memset(w_loop[:, F:W1], 0.0)
            dve.memset(zero_mat[:, :], 0.0)
            dve.memset(spread[0][:, :, :], 0.0).then_inc(cleared, 1)
            for s in range(2):
                dve.memset(rows[s][:, :, F:W1], 1.0)
                dve.memset(msg[s][:, :, F:W1], 1.0)
            step(dve.memset(ones[:, :], 1.0))
            dve.wait_ge(consts, 3)
            step(dve.tensor_scalar(ident[:, :], iota_row[:, :], row_no[:, 0:1], None, ALU.is_equal))
            step(dve.tensor_scalar(before[:, :], iota_row[:, :], row_no[:, 0:1], None, ALU.is_lt))
            step(dve.tensor_scalar(take_dst[:, :], ones[0:4, :], row_no[0:4, 0:1], 2.0, ALU.mult, ALU.is_ge))
            step(dve.tensor_scalar(take_src[:, :], ones[0:4, :], row_no[0:4, 0:1], 2.0, ALU.mult, ALU.is_lt))
            dve.wait_ge(src_in, 64)
            step(dve.tensor_scalar(tmp_i[:, :], src_i[:, :], float(R), None, ALU.mult))
            dve.tensor_tensor(typed_i[:, :], tmp_i[:, :], type_i[:, :], ALU.add).then_inc(idx0_ready, 1)
            dve.wait_ge(x_in, 32)
            dve.wait_ge(idx0_ready, 1)
            dve.sem_inc(x_ready, 1)

            dve.wait_ge(wts_in, 16 * 15)
            for t in range(NT):
                dve.wait_ge(prod_done, t + 1)
                if t >= 2:
                    dve.wait_ge(stage_out[t % 2], 16 * (t // 2))
                dve.tensor_tensor(stage[:, t % 2, :].rearrange("p (r f) -> p r f", f=F),
                                  wide[t % 2][:, :].rearrange("p (r f) -> p r f", f=F),
                                  h_bias[:, :].unsqueeze(1).to_broadcast([P, R, F]), ALU.add).then_inc(prod_used, 1)
                dve.wait_ge(prod_used, t + 3)
                dve.sem_inc(table_ready, 1)

            dve.wait_ge(dst_in, 32)
            step(dve.tensor_copy(first_f[0:1, :], dst_i[0:1, :].rearrange("p (b j) -> p b j", j=J)[:, :, 0]))
            dve.sem_inc(first_cast, 1)
            dve.wait_ge(first_bc, 1)
            step(dve.tensor_copy(first[:, :], wide[0][:, 0:NB]))
            step(dve.tensor_scalar(win_i[:, :], first[:, :], row_no[:, 0:1], None, ALU.add))
            per_block = first[:, :].unsqueeze(2).to_broadcast([P, NB, J])
            step(dve.tensor_tensor(rel[:, :].rearrange("p (b j) -> p b j", j=J),
                                   dst_i[:, :].rearrange("p (b j) -> p b j", j=J), per_block, ALU.subtract))
            step(dve.tensor_single_scalar(win_t[:, :], win_i[:, :], P - 1, ALU.bitwise_and))
            step(dve.tensor_copy(win_lo[:, :], win_t[:, :]))
            step(dve.tensor_copy(win_f[:, :], win_i[:, :]))
            step(dve.tensor_scalar(win_row[:, :], win_i[:, :], float(N - 1), None, ALU.min))
            step(dve.tensor_single_scalar(win_t[:, :], win_i[:, :], 7, ALU.arith_shift_right))
            step(dve.tensor_copy(win_hi[:, :], win_t[:, :]))
            step(dve.tensor_tensor(win_mask[:, :, :], iota_tile[:, :].unsqueeze(1).to_broadcast([P, NB, NT]),
                                   win_hi[:, :].unsqueeze(2).to_broadcast([P, NB, NT]), ALU.is_equal))
            step(dve.tensor_scalar(inside[:, :], rel[:, :], 0.0, None, ALU.is_ge))
            step(dve.tensor_scalar(outside[:, :], rel[:, :], float(WINDOW), None, ALU.is_lt))
            step(dve.tensor_tensor(inside[:, :], inside[:, :], outside[:, :], ALU.mult))
            step(dve.tensor_scalar(outside[:, :], inside[:, :], -1.0, 1.0, ALU.mult, ALU.add))
            step(dve.memset(outside[0:REPEATED, (NB - 1) * J:], 0.0))
            step(dve.tensor_reduce(any_col[:, :], outside[:, :], axis=AX, op=ALU.add))
            dve.sem_inc(any_col_ready, 1)
            step(dve.tensor_scalar(rel[:, :], rel[:, :], 1.0, None, ALU.add))
            step(dve.tensor_tensor(rel[:, :], rel[:, :], inside[:, :], ALU.mult))
            step(dve.tensor_scalar(rel[:, :], rel[:, :], -1.0, None, ALU.add))
            step(dve.memset(rel[0:REPEATED, (NB - 1) * J:], -1.0))
            step(dve.tensor_single_scalar(tmp_i[:, :], dst_i[:, :], P - 1, ALU.bitwise_and))
            step(dve.tensor_copy(far_lo[:, :], tmp_i[:, :]))
            step(dve.tensor_single_scalar(tmp_i[:, :], dst_i[:, :], 7, ALU.arith_shift_right))
            step(dve.tensor_copy(far_hi[:, :], tmp_i[:, :]))
            step(dve.tensor_scalar(far_hi[:, :], far_hi[:, :], 1.0, None, ALU.add))
            step(dve.tensor_tensor(far_hi[:, :], far_hi[:, :], outside[:, :], ALU.mult))
            step(dve.tensor_scalar(far_hi[:, :], far_hi[:, :], -1.0, None, ALU.add))
            step(dve.tensor_single_scalar(tmp_i[:, :], src_i[:, :], P - 1, ALU.bitwise_and))
            step(dve.tensor_copy(src_lo[:, :], tmp_i[:, :]))
            step(dve.tensor_single_scalar(tmp_i[:, :], src_i[:, :], 7, ALU.arith_shift_right))
            step(dve.tensor_copy(src_hi[:, :], tmp_i[:, :]))
            step(dve.tensor_copy(src_f[:, :], src_i[:, :]))
            step(dve.memset(src_f[0:REPEATED, (NB - 1) * J:], -1.0))
            step(dve.memset(src_hi[0:REPEATED, (NB - 1) * J:], -1.0))
            dve.wait_ge(any_sum, 1)
            step(dve.tensor_copy(any_i[0:1, :], wide[1][0:1, 0:1]))
            dve.sem_inc(flag_ready, 1)
            dve.wait_ge(w_in, 32)
            dve.wait_ge(ends_out, 16 * 8)

            near_blocks(GNN0, 0)
            read_sums(GNN0, NB)
            step(dve.tensor_tensor(tmp[:, :, :], x[:, :, :], agg[:, :, 0:F], ALU.add))
            layer_norm(tmp[:, :, :], x[:, :, :])
            dve.sem_inc(x_ready, 1)
            step(dve.tensor_scalar(stat[:, :], agg[:, :, F], 1.0, None, ALU.add))
            step(dve.tensor_scalar(stat2[:, :], stat[:, :], 0.0, None, ALU.is_gt))
            step(dve.tensor_scalar(dinv[:, :], stat[:, :], 1e-37, None, ALU.max))
            inverse_root(dinv)
            step(dve.tensor_tensor(dinv[:, :], dinv[:, :], stat2[:, :], ALU.mult))

            step(dve.tensor_scalar(earlier[:, :], earlier[:, :], 0.0, None, ALU.is_equal))
            step(dve.memset(earlier[0:REPEATED, (NB - 1) * J:], 0.0))
            step(dve.tensor_scalar(stat2[:, 0:1], row_no[:, 0:1], float(SLOT_ROWS), float(NT), ALU.mult, ALU.add))
            step(dve.tensor_scalar(outside[:, :], src_lo[:, :], float(SLOT_ROWS), None, ALU.mult))
            step(dve.tensor_tensor(outside[:, :], outside[:, :], src_hi[:, :], ALU.add))
            step(dve.tensor_scalar(outside[:, :], outside[:, :], stat2[:, 0:1], None, ALU.subtract))
            step(dve.tensor_tensor(outside[:, :], outside[:, :], earlier[:, :], ALU.mult))
            step(dve.tensor_scalar(scat_i[:, :], outside[:, :], stat2[:, 0:1], None, ALU.add))
            dve.sem_inc(scatter_ready, 1)

            step(dve.memset(seed[:, :, F:W1], 1.0))
            for g in range(-(-NT // 4)):
                n = min(4, NT - 4 * g)
                dve.wait_ge(prod_done, NT + g + 1)
                dve.tensor_tensor(seed[:, 4 * g:4 * g + n, 0:F], wide[g % 2][:, 0:n * F].rearrange("p (t f) -> p t f", f=F),
                                  dinv[:, 4 * g:4 * g + n].unsqueeze(2).to_broadcast([P, n, F]), ALU.mult)\
                   .then_inc(prod_used, 1)
            dve.wait_ge(prod_used, 2 + NT + -(-NT // 4))
            dve.sem_inc(table_ready, 1)
            dve.sem_inc(seed_ready, 1)
            near_blocks(GNN1, NB)
            read_sums(GNN1, 2 * NB)
            step(dve.tensor_scalar(deg_out[:, :], degs, 1.0, None, ALU.add))
            step(dve.tensor_tensor(tmp[:, :, :], agg[:, :, 0:F], rowwise(dinv[:, :]), ALU.mult))
            step(dve.tensor_tensor(tmp[:, :, :], tmp[:, :, :], featurewise(g_bias[:, :]), ALU.add))
            layer_norm(tmp[:, :, :], agg[:, :, 0:F])
            step(dve.tensor_tensor(tmp[:, :, :], agg[:, :, 0:F], featurewise(gamma[:, :]), ALU.mult))
            step(dve.tensor_tensor(tmp[:, :, :], tmp[:, :, :], featurewise(beta[:, :]), ALU.add))
            dve.sem_inc(gelu_in, 1)
            dve.wait_ge(gelu_done, 1)
            step(dve.tensor_tensor(tmp[:, :, :], x[:, :, :], xc[:, :, :], ALU.add))
            layer_norm(tmp[:, :, :], x[:, :, :])

            dve.wait_ge(table_out, 32)
            step(dve.tensor_scalar(stat[:, :], deg_out[:, :], 1.0, None, ALU.max))
            inverse_root(stat)
            step(dve.tensor_tensor(seed[:, :, 0:F], x[:, :, :], rowwise(stat[:, :]), ALU.mult))
            dve.sem_inc(table_ready, 1)
            dve.sem_inc(seed_ready, 1)
            near_blocks(GNN2, 2 * NB)
            read_sums(GNN2, 3 * NB)
            step(dve.tensor_scalar(stat[:, :], agg[:, :, F], 1.0, None, ALU.max))
            inverse_root(stat)
            step(dve.tensor_tensor(tmp[:, :, :], agg[:, :, 0:F], rowwise(stat[:, :]), ALU.mult))
            step(dve.tensor_tensor(tmp[:, :, :], tmp[:, :, :], x[:, :, :], ALU.add))
            layer_norm(tmp[:, :, :], x[:, :, :])

            dve.sem_inc(table_ready, 1)
            dve.sem_inc(seed_ready, 1)
            dve.wait_ge(hi_ready, 1)
            step(dve.tensor_tensor(tmp[:, :, :], x[:, :, :], x_parts[:, :, 0, :], ALU.subtract))
            dve.sem_inc(rest_ready, 1)
            dve.wait_ge(mid_ready, 1)
            step(dve.tensor_tensor(x_parts[:, :, 2, :], tmp[:, :, :], x_parts[:, :, 1, :], ALU.subtract))
            dve.sem_inc(parts_ready, 1)
            dve.wait_ge(table_out, 64)
            dve.wait_ge(parts_out, 32)
            attend_way(dve, attend_blocks)
            dve.wait_ge(final_in, 16 * 2 * TRIO)
            for k in (1, 3, 5):
                step(dve.tensor_tensor(finals[k - 1][:, 0:NT, :], finals[k - 1][:, 0:NT, :], finals[k][:, 0:NT, :], ALU.add))
            step(dve.tensor_tensor(finals[0][:, 0:NT, :], finals[0][:, 0:NT, :], finals[2][:, 0:NT, :], ALU.add))
            step(dve.tensor_tensor(agg[:, :, :], finals[0][:, 0:NT, :], finals[4][:, 0:NT, :], ALU.add))
            step(dve.tensor_scalar(stat[:, :], agg[:, :, F], 0.0, None, ALU.is_gt))
            step(dve.tensor_scalar(stat2[:, :], stat[:, :], -1.0, 1.0, ALU.mult, ALU.add))
            step(dve.tensor_tensor(stat[:, :], stat[:, :], agg[:, :, F], ALU.mult))
            step(dve.tensor_tensor(stat[:, :], stat[:, :], stat2[:, :], ALU.add))
            step(dve.reciprocal(stat[:, :], stat[:, :]))
            step(dve.tensor_tensor(tmp[:, :, :], agg[:, :, 0:F], rowwise(stat[:, :]), ALU.mult))
            step(dve.tensor_tensor(tmp[:, :, :], tmp[:, :, :], x[:, :, :], ALU.add))
            layer_norm(tmp[:, :, :], x[:, :, :])
            dve.sem_inc(table_ready, 1)


INPUTS = ["x", "src", "dst", "edge_attr_64", "edge_type_8", "edge_weight1", "L0_gnn_weight", "L0_gnn_h_bias",
          "L0_gnn_loop_weight", "L1_gnn_W", "L1_gnn_b", "L1_gnn_gamma", "L1_gnn_beta", "L3_gnn_W1", "L3_gnn_b1",
          "L3_gnn_W2", "L3_gnn_b2", "L3_gnn_linear_coef"]


def kernel(**inputs):
    import numpy as np
    import concourse.bacc as bacc
    from concourse.bass_utils import run_bass_kernel_spmd

    nc = bacc.Bacc("TRN2", target_bir_lowering=False, num_devices=1)
    arrays, A = {}, {}
    for name in INPUTS:
        a = np.ascontiguousarray(inputs[name])
        arrays["in_" + name] = a
        A[name] = nc.dram_tensor("in_" + name, a.shape, mybir.dt.from_np(a.dtype), kind="ExternalInput").ap()
    out = nc.dram_tensor("out_0", (N, F), F32, kind="ExternalOutput").ap()
    build(nc, A, out)
    result = run_bass_kernel_spmd(nc, [arrays], core_ids=[0])
    return result.results[0]["out_0"]
```

```python
import concourse.bass as bass
from concourse import mybir

N = 3125
F = 64
E = 103125
R = 8
P = 128
NT = -(-N // P)
TAIL = N - (NT - 1) * P
J = 15
BE = P * J
NB = -(-E // BE)
assert NB % 2 == 0
LAST = E - BE
REPEATED = ((NB - 1) * BE - LAST) // J
assert REPEATED * J == (NB - 1) * BE - LAST
LOOKED_UP = [0, 2, 2]
WINDOW = 128
W1 = F + 1
BANK_TILES = [(0, 7), (7, 14), (14, 21), (21, NT)]
PAIRS = [(0, 1, 2), (3, 4, 5), (6, 7)]
TRIO = 3
TRIOS = J // TRIO
assert TRIOS % 2 == 1
SLOT_ROWS = NT + 1
EPS = 1e-5
STAGE_TILES = 3
STAGES = -(-NT // STAGE_TILES)

F32 = mybir.dt.float32
BF16 = mybir.dt.bfloat16
I32 = mybir.dt.int32
ALU = mybir.AluOpType
ACT = mybir.ActivationFunctionType
AX = mybir.AxisListType.X
GNN0, GNN1, GNN2, GNN3 = range(4)


def build(nc, A, out):
    def sb(name, shape, dt=F32):
        return nc.alloc_sbuf_tensor(name, list(shape), dt)

    def sem(name):
        return nc.alloc_semaphore(name)

    table = [nc.dram_tensor("table_typed", (N * R, F), F32, kind="Internal").ap(),
             nc.dram_tensor("table_gcn", (N, F), F32, kind="Internal").ap(),
             nc.dram_tensor("table_sym", (N, F), F32, kind="Internal").ap(),
             nc.dram_tensor("table_attn", (N, F), F32, kind="Internal").ap()]
    table_parts = nc.dram_tensor("table_parts", ((NT + 1) * P, 3 * F), BF16,
                                 kind="Internal").ap()
    scattered = [[nc.dram_tensor(f"scattered{g}_{k}", (P * SLOT_ROWS, W1), F32, kind="Internal").ap()
                  for k in range(TRIO)] for g in range(2)]
    ends = nc.dram_tensor("ends", (4, NB, BE), BF16, kind="Internal").ap()

    iota_row = sb("iota_row", [P, P])
    iota_tile = sb("iota_tile", [P, NT])
    node_no = sb("node_no", [P, NT])
    row_no = sb("row_no", [P, 1])
    ident = sb("ident", [P, P])
    ones = sb("ones", [P, P])
    zero_mat = sb("zero_mat", [P, P])

    src_i = sb("src_i", [P, NB * J], I32)
    dst_i = sb("dst_i", [P, NB * J], I32)
    type_i = sb("type_i", [P, NB * J], I32)
    typed_i = sb("typed_i", [P, NB * J], I32)
    weight = sb("weight", [P, NB * J])
    tmp_i = sb("tmp_i", [P, NB * J], I32)
    rel = sb("rel", [P, NB * J])
    src_lo = sb("src_lo", [P, NB * J])
    src_hi = sb("src_hi", [P, NB * J])
    far_lo = sb("far_lo", [P, NB * J])
    far_hi = sb("far_hi", [P, NB * J])
    outside = sb("outside", [P, NB * J])
    src_f = sb("src_f", [P, NB * J])
    earlier = sb("earlier", [P, NB * J])
    inside = earlier
    scat_i = sb("scat_i", [P, NB * J], I32)
    first_f = sb("first_f", [1, NB])
    first = sb("first", [P, NB])
    win_i = sb("win_i", [P, NB], I32)
    win_t = sb("win_t", [P, NB], I32)
    win_lo = sb("win_lo", [P, NB])
    win_hi = sb("win_hi", [P, NB])
    win_mask = sb("win_mask", [P, NB, NT])
    win_f = sb("win_f", [P, NB])
    any_col = sb("any_col", [P, 1])
    any_i = sb("any_i", [1, 1], I32)

    x = sb("x", [P, NT, F])
    scratch = sb("scratch", [P, NT * (F + W1)])
    xc = scratch[:, 0:NT * F].rearrange("p (t f) -> p t f", f=F)
    tmp = sb("tmp", [P, NT, F])
    agg = scratch[:, NT * F:].rearrange("p (t f) -> p t f", f=W1)
    x_parts = scratch[:, 0:NT * 3 * F // 2].bitcast(BF16).rearrange("p (t k f) -> p t k f", k=3, f=F)
    seed = sb("seed", [P, NT, W1])
    stat = sb("stat", [P, NT])
    stat2 = sb("stat2", [P, NT])
    dinv = sb("dinv", [P, NT])
    deg_out = sb("deg_out", [P, NT])

    w_types = sb("w_types", [F + 1, R, F])
    w_loop = sb("w_loop", [F, W1])
    w_gcn = sb("w_gcn", [F, F])
    h_bias = sb("h_bias", [P, F])
    g_bias = sb("g_bias", [P, F])
    gamma = sb("gamma", [P, F])
    beta = sb("beta", [P, F])
    mlp1 = sb("mlp1", [P, P])
    mlp2 = sb("mlp2", [P, P])
    mlp_b1 = sb("mlp_b1", [P, 1])
    mlp_b2 = sb("mlp_b2", [P, F])
    coef = sb("coef", [P, F])

    idx = sb("idx", [P, 2, J], I32)
    rows = [sb(f"rows{s}", [P, J, W1]) for s in range(2)]
    msg = [sb(f"msg{s}", [P, J, W1]) for s in range(2)]
    hot = [sb(f"hot{s}", [P, J, P]) for s in range(2)]
    far_idx = sb("far_idx", [P, 2, J], I32)
    attn = sb("attn", [P, 2, J])
    weighted = sb("weighted", [P, J, W1])
    ends_row = [sb(f"ends_row{s}", [4, BE], BF16) for s in range(2)]
    take_src = sb("take_src", [4, P], BF16)
    take_dst = sb("take_dst", [4, P], BF16)
    before = sb("before", [P, P])
    win_x = [sb(f"win_x{s}", [P, 3 * F], BF16) for s in range(2)]
    whole = [h[:, :, :].rearrange("p j e -> p (j e)") for h in hot]
    ends_i = whole[0][0:NB, :].bitcast(I32)
    ends_ab = [whole[1][0:NB, k * BE // 2:(k + 1) * BE // 2].bitcast(BF16) for k in range(2)]
    logit = sb("logit", [P, 2, J])
    prod = sb("prod", [P, J, F])
    mlp_out = [sb(f"mlp_out{s}", [P, J, F]) for s in range(2)]
    repeated = [m[0:1, :, :].rearrange("p j f -> p (j f)").bitcast(BF16)[:, 0:REPEATED * J] for m in mlp_out]
    ea = [sb(f"ea{s}", [P, J * F]) for s in range(2)]
    eaT = [sb(f"eaT{u}", [P, 3 * P]) for u in range(3)]
    hidT = [sb(f"hidT{u}", [P, 3 * P]) for u in range(3)]
    spread = [sb(f"spread{s}", [P, SLOT_ROWS, W1]) for s in range(2)]
    spread_hot = sb("spread_hot", [P, 2, P])
    far_mask = sb("far_mask", [P, 2, NT])
    shared = sb("shared", [P, 2 * J * P])
    halves = [shared[:, s * J * P:(s + 1) * J * P] for s in range(2)]
    xT = shared[0:F + 1, 0:NT * P]
    stage = [a[:, :, :].rearrange("p t f -> p (t f)")[:, 0:STAGE_TILES * R * F] for a in (tmp, agg, seed, xc, spread[1])]
    dst_hot = [halves[0][:, s * J * P // 2:(s + 1) * J * P // 2].bitcast(BF16).rearrange("p (j e) -> p j e", e=P)
               for s in range(2)]
    far_x = [halves[0][:, s * J * F:(s + 1) * J * F].rearrange("p (j f) -> p j f", f=F) for s in range(2)]
    parts = [a[:, 0:3 * J * W1 // 2 + 1].bitcast(BF16)[:, 0:3 * J * W1].rearrange("p (k j f) -> p k j f", k=3, f=W1)
             for a in (halves[1], seed[:, :, :].rearrange("p t f -> p (t f)"))]
    src_same = [h[:, 0:J * P // 2].bitcast(BF16).rearrange("p (j e) -> p j e", e=P) for h in whole]
    same = [h.rearrange("p (j e) -> p j e", e=P) for h in halves]
    src_hot = [shared[:, s * J * P // 2:(s + 1) * J * P // 2].bitcast(BF16).rearrange("p (j e) -> p j e", e=P)
               for s in range(2)]
    lookup = [halves[1 - c][:, 0:NT * P // 2].bitcast(BF16).rearrange("p (t e) -> p t e", e=P) for c in range(2)]
    act_lookup = tmp[:, :, :].rearrange("p t f -> p (t f)")[:, 0:NT * P // 2].bitcast(BF16)\
        .rearrange("p (t e) -> p t e", e=P)
    src_tile = [sb(f"src_tile{s}", [P, J, NT], BF16) for s in range(2)]

    sums = [nc.alloc_psum_tensor(f"sums{g}", [P, 512], F32) for g in range(4)]
    bank_t = nc.alloc_psum_tensor("bank_t", [P, 512], F32)
    bank_h = nc.alloc_psum_tensor("bank_h", [P, 512], F32)
    wide = [nc.alloc_psum_tensor(f"wide{g}", [P, 512], F32) for g in range(2)]
    part = [bank_t[:, 384:384 + W1], bank_h[:, 384:384 + W1]]
    chunk_src = [wide[1 - c][:, 0:P] for c in range(2)]
    found = [wide[1 - c][:, 256:256 + 3 * F] for c in range(2)]
    act_src = [b[:, 0:P] for b in (bank_t, bank_h)]
    act_found = [b[:, P:P + 3 * F] for b in (bank_t, bank_h)]
    degs = wide[0][:, 0:NT]

    src_in, dst_in, x_in, wts_in, w_in = sem("src_in"), sem("dst_in"), sem("x_in"), sem("wts_in"), sem("w_in")
    consts = sem("consts")
    zeroed = sem("zeroed")
    dve_step = sem("dve_step")
    first_cast = sem("first_cast")
    first_bc = sem("first_bc")
    any_sum = sem("any_sum")
    any_col_ready = sem("any_col_ready")
    flag_ready = sem("flag_ready")
    idx0_ready = sem("idx0_ready")
    x_ready = sem("x_ready")
    tr_done = sem("tr_done")
    tr_copied = sem("tr_copied")
    prod_done = sem("prod_done")
    prod_used = sem("prod_used")
    stage_out = [sem(f"stage_out{g}") for g in range(len(stage))]
    types_in = sem("types_in")
    bias_ready = sem("bias_ready")
    seed_ready = sem("seed_ready")
    table_ready = sem("table_ready")
    table_out = sem("table_out")
    out_done = sem("out_done")
    src_hot_ready = sem("src_hot_ready")
    src_hot_used = sem("src_hot_used")
    src_cast = sem("src_cast")
    act_src_cast = sem("act_src_cast")
    lookup_ready = sem("lookup_ready")
    tmp_free = sem("tmp_free")
    distances = sem("distances")
    act_lookup_ready = sem("act_lookup_ready")
    rows_found = sem("rows_found")
    rows_put = sem("rows_put")
    root_in, root_done = sem("root_in"), sem("root_done")
    gelu_in, gelu_done = sem("gelu_in"), sem("gelu_done")

    ends_loaded = sem("ends_loaded")
    ends_cast = sem("ends_cast")
    ends_out = sem("ends_out")
    cleared = sem("cleared")
    landed = [sem("landed0"), sem("landed1")]
    scatter_ready = sem("scatter_ready")
    pool_seen = sem("pool_seen")
    hi_ready, mid_ready = sem("hi_ready"), sem("mid_ready")
    rest_ready = sem("rest_ready")
    parts_ready = sem("parts_ready")
    parts_out = sem("parts_out")
    final_in = [sem(f"final_in{k}") for k in range(TRIO)]

    class Sems:

        def __init__(self, way):
            self.rows_in = [sem(f"{way}_rows_in{s}") for s in range(2)]
            self.idx_staged = sem(f"{way}_idx_staged")
            self.ends_in = [sem(f"{way}_ends_in{s}") for s in range(2)]
            self.broadcast = sem(f"{way}_broadcast")
            self.compared = sem(f"{way}_compared")

    class SumSems(Sems):

        def __init__(self, way):
            super().__init__(way)
            self.main_done = sem(f"{way}_main_done")
            self.hot_ready = sem(f"{way}_hot_ready")
            self.spread_ready = sem(f"{way}_spread_ready")
            self.merged = sem(f"{way}_merged")
            self.mask_done = sem(f"{way}_mask_done")

    class AttendSems(Sems):

        def __init__(self, way):
            super().__init__(way)
            self.windowed = True
            self.win_in = [sem(f"{way}_win_in{s}") for s in range(2)]
            self.ea_in = [sem(f"{way}_ea_in{s}") for s in range(2)]
            self.taken = sem(f"{way}_taken")
            self.part_ready = sem(f"{way}_part_ready")
            self.part_cast = sem(f"{way}_part_cast")
            self.weighted = sem(f"{way}_weighted")
            self.seen = sem(f"{way}_seen")
            self.seen_copied = sem(f"{way}_seen_copied")
            self.blocks_in = sem(f"{way}_blocks_in")
            self.msg_done = sem(f"{way}_msg_done")
            self.prod_ready = sem(f"{way}_prod_ready")
            self.logit_ready = sem(f"{way}_logit_ready")
            self.attn_ready = sem(f"{way}_attn_ready")
            self.t_ready = sem(f"{way}_t_ready")
            self.t_copied = sem(f"{way}_t_copied")
            self.h_ready = sem(f"{way}_h_ready")
            self.hid_ready = sem(f"{way}_hid_ready")
            self.unit_done = sem(f"{way}_unit_done")
            self.mlp_copied = sem(f"{way}_mlp_copied")

    near, far, attend = SumSems("near"), SumSems("far"), AttendSems("attend")
    SLOTS = 2
    FAR_SLOTS = 2 * J

    def bank_of(banks, s, n, S):
        return banks[(s * casts_of(S) + n) % 2]

    def casts_of(S):
        return TRIOS if S is near or not S.windowed else 2 * TRIOS

    finals = [t[:, :, :] for t in spread]
    for big in (*whole, *halves):
        finals.append(big[:, 0:SLOT_ROWS * W1].rearrange("p (t f) -> p t f", f=W1))

    def edges(a):
        return a[0:(NB - 1) * BE].rearrange("(b p j) -> p b j", p=P, j=J)

    def gathered(layer):
        return J - LOOKED_UP[layer]

    def index_of(layer):
        return typed_i if layer == GNN0 else src_i

    def blocks(eng, body, peel):
        if peel:
            with eng.Fori(0, NB // 2 - 1) as i:
                body(i, False)
            body(NB // 2 - 1, True)
        else:
            with eng.Fori(0, NB // 2) as i:
                body(i, False)

    def attend_way(eng, run):
        count = eng.value_load(any_i[0:1, 0:1], min_val=0, max_val=NB * BE)
        with eng.If(count > 0):
            attend.windowed = False
            run(attend)
        with eng.Else():
            attend.windowed = True
            run(attend)

    def far_way(eng, run):
        count = eng.value_load(any_i[0:1, 0:1], min_val=0, max_val=NB * BE)
        with eng.If(count > 0):
            run()

    with nc.Block() as block:

        @block.sync
        def _(sp):
            sp.dma_start(w_types[0:F, :, :], A["L0_gnn_weight"].rearrange("r i o -> i r o")).then_inc(types_in, 16)
            sp.dma_start(h_bias[:, :], A["L0_gnn_h_bias"].partition_broadcast(P)).then_inc(types_in, 16)
            sp.dma_start(w_loop[:, 0:F], A["L0_gnn_loop_weight"]).then_inc(types_in, 16)
            flat_w = A["edge_weight1"].rearrange("e o -> (e o)")
            for t, a, s in ((dst_i, A["dst"], dst_in), (src_i, A["src"], src_in),
                            (type_i, A["edge_type_8"], src_in)):
                sp.dma_start(t[:, 0:(NB - 1) * J].rearrange("p (b j) -> p b j", j=J), edges(a)).then_inc(s, 16)
                sp.dma_start(t[:, (NB - 1) * J:], a[LAST:E].rearrange("(p j) -> p j", j=J)).then_inc(s, 16)
            sp.dma_start(weight[:, 0:(NB - 1) * J].rearrange("p (b j) -> p b j", j=J), edges(flat_w))\
              .then_inc(w_in, 16)
            sp.dma_start(weight[:, (NB - 1) * J:], flat_w[LAST:E].rearrange("(p j) -> p j", j=J)).then_inc(w_in, 16)

            for g in range(STAGES):
                t0, t1 = g * STAGE_TILES, min(NT, (g + 1) * STAGE_TILES)
                n = P if t1 < NT else TAIL
                assert n == P or t1 - t0 == 1
                sp.wait_ge(prod_used, 2 + t1)
                sp.dma_start(table[GNN0][t0 * P * R:(t0 * P + (t1 - t0 - 1) * P + n) * R, :]
                             .rearrange("(t p r) f -> p t (r f)", p=n, r=R),
                             stage[g % len(stage)][0:n, 0:(t1 - t0) * R * F].rearrange("p (t q) -> p t q", q=R * F))\
                  .then_inc(stage_out[g % len(stage)], 16)

            sp.wait_ge(ends_out, 16 * 12)

            def ends_load(i, last):
                for s in range(2):
                    sp.wait_ge(near.broadcast, TRIOS * (2 * i + s) + TRIOS)
                    sp.dma_start(ends_row[s][:, :], ends[:, bass.ds(2 * i + s, 1), :].rearrange("r b e -> r (b e)"))\
                      .then_inc(near.ends_in[s], 16)
            blocks(sp, ends_load, False)

            def attributes(v, s, start):
                sp.dma_start(ea[s][:, :], A["edge_attr_64"][bass.ds(start, BE), :]
                             .rearrange("(p j) f -> p (j f)", j=J)).then_inc(attend.ea_in[s], 16)

            def block_ends(v, s):
                sp.dma_start(ends_row[s][:, :], ends[:, bass.ds(v, 1), :].rearrange("r b e -> r (b e)"))\
                  .then_inc(attend.ends_in[s], 16)

            def window(v, s):
                first_node = sp.value_load(win_i[0:1, bass.ds(v, 1)], min_val=0, max_val=N - 1)
                sp.dma_start(win_x[s][:, :], table_parts[bass.ds(first_node, P), :]).then_inc(attend.win_in[s], 16)

            def store_table(layer, source):
                sp.dma_start(table[layer][0:(NT - 1) * P, :].rearrange("(t p) f -> p t f", p=P),
                             source[:, 0:NT - 1, 0:F]).then_inc(table_out, 16)
                sp.dma_start(table[layer][(NT - 1) * P:N, :], source[0:TAIL, NT - 1, 0:F]).then_inc(table_out, 16)

            for s in range(2):
                attributes(s, s, s * BE)
            sp.wait_ge(near.broadcast, TRIOS * (NB + SLOTS))
            for layer in (GNN1, GNN2):
                sp.wait_ge(table_ready, layer)
                store_table(layer, seed)

                def lookup_ends(i, last):
                    for s in range(2):
                        v = 2 * i + s
                        sp.wait_ge(src_cast, (layer - 1) * NB + v + 1)
                        sp.dma_start(ends_row[s][:, :], ends[:, bass.ds(v, 1), :].rearrange("r b e -> r (b e)"))\
                          .then_inc(near.ends_in[s], 16)
                blocks(sp, lookup_ends, False)
            sp.wait_ge(src_cast, 2 * NB + SLOTS)
            for s in range(2):
                block_ends(s, s)
            sp.wait_ge(parts_ready, 1)
            sp.dma_start(table_parts[0:(NT - 1) * P, :].rearrange("(t p) f -> p t f", p=P),
                         x_parts[:, 0:NT - 1, :, :].rearrange("p t k f -> p t (k f)")).then_inc(parts_out, 16)
            for t in (NT - 1, NT):
                sp.dma_start(table_parts[t * P:(t + 1) * P, :],
                             x_parts[:, NT - 1, :, :].rearrange("p k f -> p (k f)")).then_inc(parts_out, 16)

            def block_loads(S):
                def load(v, s, start):
                    sp.wait_ge(S.unit_done, 3 * v + 3)
                    attributes(v, s, start)
                    sp.wait_ge(S.broadcast, casts_of(S) * v + casts_of(S))
                    block_ends(v, s)
                    if S.windowed:
                        window(v, s)

                if S.windowed:
                    window(0, 0)
                    window(1, 1)
                else:
                    store_table(GNN3, x)
                with sp.Fori(1, NB // 2 - 1) as i:
                    load(2 * i, 0, i * (2 * BE))
                    load(2 * i + 1, 1, i * (2 * BE) + BE)
                load(NB - 2, 0, (NB - 2) * BE)
                load(NB - 1, 1, LAST)

            sp.wait_ge(flag_ready, 1)
            sp.wait_ge(parts_out, 48)
            attend_way(sp, block_loads)
            for g in range(2):
                sp.wait_ge(landed[g], 16 * TRIO * (1 + NB * TRIOS // 2))
                for k in range(TRIO):
                    sp.dma_start(finals[g * TRIO + k].rearrange("p t f -> p (t f)"),
                                 scattered[g][k].rearrange("(p t) f -> p (t f)", p=P)).then_inc(final_in[k], 16)

            sp.wait_ge(table_ready, 4)
            sp.dma_start(out[0:(NT - 1) * P, :].rearrange("(t p) f -> p t f", p=P), x[:, 0:NT - 1, :])\
              .then_inc(out_done, 16)
            sp.dma_start(out[(NT - 1) * P:N, :], x[0:TAIL, NT - 1, :]).then_inc(out_done, 16)
            sp.wait_ge(out_done, 32)

        @block.gpsimd
        def _(pool):
            pool.iota(iota_row[:, :], pattern=[[1, P]], base=0, channel_multiplier=0,
                      allow_small_or_imprecise_dtypes=True).then_inc(consts, 1)
            pool.iota(iota_tile[:, :], pattern=[[1, NT]], base=0, channel_multiplier=0,
                      allow_small_or_imprecise_dtypes=True).then_inc(consts, 1)
            pool.iota(row_no[:, :], pattern=[[0, 1]], base=0, channel_multiplier=1,
                      allow_small_or_imprecise_dtypes=True).then_inc(consts, 1)

            def gathers(layer, S, v0):
                def body(i, last):
                    for s in range(2):
                        v = 2 * i + s
                        if S is near:
                            pool.wait_ge(S.idx_staged, v0 + v + 1)
                            pool.sem_inc(pool_seen, 1)
                        else:
                            pool.wait_ge(S.merged, (v0 + v) * J + J)
                            pool.tensor_copy(idx[:, s, :], index_of(layer)[:, bass.ds(v * J, J)]).then_inc(S.idx_staged, 1)
                            pool.wait_ge(S.idx_staged, 1)
                            pool.sem_clear(S.idx_staged)
                        for j in range(gathered(layer) if S is near else J):
                            pool.indirect_dma_start(
                                out=rows[s][:, j, 0:F], out_offset=None, in_=table[layer][:, :],
                                in_offset=bass.IndirectOffsetOnAxis(ap=idx[:, s, j:j + 1], axis=0),
                            ).then_inc(S.rows_in[s], 16)
                blocks(pool, body, False)

            for n, name in enumerate(("src", "dst")):
                if n:
                    pool.wait_ge(ends_cast, 1)
                pool.dma_start(ends_i[0:NB - 1, :], A[name][0:(NB - 1) * BE].rearrange("(b e) -> b e", e=BE))\
                    .then_inc(ends_loaded, 16)
                pool.dma_start(ends_i[NB - 1:NB, :], A[name][LAST:E].rearrange("(o e) -> o e", o=1)).then_inc(ends_loaded, 16)
                pool.wait_ge(ends_cast, n + 1)
                for k in range(2):
                    row = ends[2 * n + k]
                    pool.dma_start(row[0:NB - 1, :], ends_ab[k][0:NB - 1, :]).then_inc(ends_out, 16)
                    pool.dma_start(row[NB - 1:NB, REPEATED * J:], ends_ab[k][NB - 1:NB, REPEATED * J:]).then_inc(ends_out, 16)
                    pool.dma_start(row[NB - 1:NB, 0:REPEATED * J], repeated[k]).then_inc(ends_out, 16)
            pool.wait_ge(cleared, 1)
            for g in range(2):
                for k in range(TRIO):
                    pool.dma_start(scattered[g][k].rearrange("(p t) f -> p (t f)", p=P),
                                   spread[0][:, :, :].rearrange("p t f -> p (t f)")).then_inc(landed[g], 16)
            pool.wait_ge(idx0_ready, 1)
            for layer in range(3):
                if layer == GNN0:
                    for g in range(len(stage)):
                        pool.wait_ge(stage_out[g], 16 * (1 + (STAGES - 1 - g) // len(stage)))
                else:
                    pool.wait_ge(table_out, 32 * layer)
                gathers(layer, near, layer * NB)
                if layer == GNN0:
                    pool.wait_ge(flag_ready, 1)
                pool.wait_ge(near.main_done, SLOTS + (layer + 1) * NB)
                far_way(pool, lambda: gathers(layer, far, layer * NB))

            def scatters(S):
                def fetch(s, v):
                    if S.windowed:
                        return
                    pool.tensor_copy(far_idx[:, s, :], dst_i[:, bass.ds(v * J, J)]).then_inc(S.idx_staged, 1)
                    pool.wait_ge(S.idx_staged, 1)
                    pool.sem_clear(S.idx_staged)
                    for j in range(J):
                        pool.indirect_dma_start(
                            out=far_x[s][:, j, :], out_offset=None, in_=table[GNN3][:, :],
                            in_offset=bass.IndirectOffsetOnAxis(ap=far_idx[:, s, j:j + 1], axis=0)).then_inc(S.rows_in[s], 16)

                def body(i, last):
                    for s in range(2):
                        v = 2 * i + s
                        for q in range(TRIOS):
                            n = s * TRIOS + q
                            pool.wait_ge(S.seen_copied, v * TRIOS + q + 1 + SLOTS)
                            pool.sem_inc(pool_seen, 1)
                            if q == 0 and not last:
                                fetch(s, v + 2)
                            pool.wait_ge(landed[n % 2], i * (16 * TRIO * TRIOS) + 16 * TRIO * (n // 2 + 1))
                            pool.sem_inc(pool_seen, 1)
                            if q == 1:
                                pool.sem_inc(S.blocks_in, 1)
                            for k in range(TRIO):
                                j = q * TRIO + k
                                pool.indirect_dma_start(
                                    out=scattered[n % 2][k][:, :],
                                    out_offset=bass.IndirectOffsetOnAxis(ap=idx[:, s, j:j + 1], axis=0),
                                    in_=rows[s][:, j, :], in_offset=None, compute_op=ALU.add).then_inc(landed[n % 2], 16)
                pool.sem_inc(S.blocks_in, 1)
                if not S.windowed:
                    pool.wait_ge(table_out, 32 * GNN3)
                fetch(0, 0)
                fetch(1, 1)
                blocks(pool, body, True)

            pool.wait_ge(scatter_ready, 1)
            attend_way(pool, scatters)

        @block.scalar
        def _(act):
            act.dma_start(x[:, 0:NT - 1, :], A["x"][0:(NT - 1) * P, :].rearrange("(t p) f -> p t f", p=P))\
               .then_inc(x_in, 16)
            act.wait_ge(zeroed, 1)
            act.dma_start(x[0:TAIL, NT - 1, :], A["x"][(NT - 1) * P:N, :]).then_inc(x_in, 16)
            act.dma_start(w_gcn[:, :], A["L1_gnn_W"]).then_inc(wts_in, 16)
            for t, name in ((g_bias, "L1_gnn_b"), (gamma, "L1_gnn_gamma"), (beta, "L1_gnn_beta"), (mlp_b2, "L3_gnn_b2")):
                act.dma_start(t[:, :], A[name].partition_broadcast(P)).then_inc(wts_in, 16)
            act.dma_start(coef[:, :], A["L3_gnn_linear_coef"].rearrange("f o -> (f o)").partition_broadcast(P))\
               .then_inc(wts_in, 16)
            for h in range(2):
                q = slice(h * F, (h + 1) * F)
                act.dma_start(mlp1[q, q], A["L3_gnn_W1"]).then_inc(wts_in, 16)
                act.dma_start(mlp2[q, q], A["L3_gnn_W2"]).then_inc(wts_in, 16)
                act.dma_start(mlp_b1[q, :], A["L3_gnn_b1"].rearrange("(f o) -> f o", o=1)).then_inc(wts_in, 16)

            def copy_transposed(base):
                for g in range(-(-NT // 4)):
                    n = min(4, NT - 4 * g) * P
                    act.wait_ge(tr_done, base + g + 1)
                    act.activation(xT[0:F, 4 * g * P:4 * g * P + n], (bank_t, bank_h)[g % 2][0:F, 0:n], ACT.Copy)\
                       .then_inc(tr_copied, 1)

            roots = [0]

            def root(a):
                roots[0] += 1
                act.wait_ge(root_in, roots[0])
                act.activation(a[:, :], a[:, :], ACT.Sqrt).then_inc(root_done, 1)

            def look_up(n, s):
                act.wait_ge(act_src_cast, n + 1)
                for t in range(NT):
                    last = act.activation(act_lookup[:, t, :], act_src[s], ACT.Abs, bias=node_no[:, t:t + 1], scale=-1.0)
                last.then_inc(distances, 1)
                act.wait_ge(distances, n + 1)
                act.activation(act_lookup, act_lookup, ACT.Relu, bias=ones[:, 0:1], scale=-1.0).then_inc(act_lookup_ready, 1)

            def stage_idx(layer):
                def body(i, last):
                    for s in range(2):
                        v = 2 * i + s
                        act.wait_ge(near.main_done, layer * NB + v + 1)
                        act.activation(idx[:, s, :], index_of(layer)[:, bass.ds(v * J, J)], ACT.Copy).then_inc(near.idx_staged, 1)
                        if LOOKED_UP[layer]:
                            look_up((layer - 1) * NB + v, s)
                if LOOKED_UP[layer]:
                    act.wait_ge(tmp_free, layer)
                blocks(act, body, False)

            def transposed(v, u):
                n = len(PAIRS[u]) * P
                act.wait_ge(attend.t_ready, 3 * v + u + 1)
                act.activation(eaT[u][:, 0:n], bank_t[:, 0:n], ACT.Copy).then_inc(attend.t_copied, 1)

            def hidden(v, u):
                n = len(PAIRS[u]) * P
                act.wait_ge(attend.h_ready, 3 * v + u + 1)
                act.wait_ge(attend.unit_done, 3 * v + u + 4)
                act.activation(hidT[u][:, 0:n], bank_h[:, 0:n], ACT.Tanh, bias=mlp_b1[:, 0:1])\
                   .then_inc(attend.hid_ready, 1)

            copy_transposed(0)
            for t in range(NT):
                g = t // STAGE_TILES
                act.wait_ge(prod_done, t + 1)
                if t % STAGE_TILES == 0 and g >= len(stage):
                    act.wait_ge(stage_out[g % len(stage)], 16 * (g // len(stage)))
                act.activation(stage[g % len(stage)][:, t % STAGE_TILES * R * F:(t % STAGE_TILES + 1) * R * F],
                               wide[t % 2][:, :], ACT.Copy).then_inc(prod_used, 1)
            act.wait_ge(idx0_ready, 1)
            stage_idx(GNN0)
            root(stat2)
            copy_transposed(-(-NT // 4))
            root(dinv)
            stage_idx(GNN1)
            root(stat2)
            act.wait_ge(gelu_in, 1)
            act.activation(xc[:, :, :], tmp[:, :, :], ACT.Gelu).then_inc(gelu_done, 1)
            root(stat2)
            root(stat)
            stage_idx(GNN2)
            act.wait_ge(wts_in, 16 * 12)
            transposed(0, 0)
            hidden(0, 0)
            root(stat)
            for v, u in ((0, 1), (0, 2), (1, 0)):
                transposed(v, u)
                hidden(v, u)
            root(stat2)

            def mlp(S):
                def weighted_part(v, s, k):
                    act.wait_ge(S.part_ready, 2 * v + k + 1)
                    act.activation(parts[s][:, k, :, :], weighted[:, :, :], ACT.Copy).then_inc(S.part_cast, 1)

                def body(i, last):
                    for s in range(2):
                        v = 2 * i + s
                        ahead = not (last and s == 1)
                        act.wait_ge(S.logit_ready, v + 1)
                        act.activation(attn[:, s, :], logit[:, s, :], ACT.Exp).then_inc(S.attn_ready, 1)
                        if ahead:
                            transposed(v + 1, 1)
                        weighted_part(v, s, 0)
                        if ahead:
                            hidden(v + 1, 1)
                            transposed(v + 1, 2)
                        weighted_part(v, s, 1)
                        if ahead:
                            hidden(v + 1, 2)
                        if not last:
                            transposed(v + 2, 0)
                        act.wait_ge(S.blocks_in, v + 1)
                        act.activation(idx[:, s, :], scat_i[:, bass.ds(v * J, J)], ACT.Copy)
                        for q in range(TRIOS):
                            act.wait_ge(S.seen, v * TRIOS + q + 1)
                            act.activation(rows[s][:, q * TRIO:(q + 1) * TRIO, :],
                                           sums[2 + (s + q) % 2][:, 0:TRIO * W1].rearrange("p (j f) -> p j f", f=W1),
                                           ACT.Copy).then_inc(S.seen_copied, 1)
                        if not last:
                            hidden(v + 2, 0)
                blocks(act, body, True)

            act.wait_ge(table_ready, GNN3)
            act.activation(x_parts[:, :, 0, :], x[:, :, :], ACT.Copy).then_inc(hi_ready, 1)
            act.wait_ge(rest_ready, 1)
            act.activation(x_parts[:, :, 1, :], tmp[:, :, :], ACT.Copy).then_inc(mid_ready, 1)
            act.wait_ge(flag_ready, 1)
            attend_way(act, mlp)
            root(stat2)

        @block.tensor
        def _(pe):
            pe.sem_inc(near.main_done, SLOTS)
            pe.sem_inc(near.merged, SLOTS)
            pe.sem_inc(far.merged, FAR_SLOTS)
            pe.sem_inc(src_hot_used, SLOTS)
            pe.sem_inc(src_cast, SLOTS)
            pe.sem_inc(attend.unit_done, SLOTS * len(PAIRS))
            pe.sem_inc(near.broadcast, SLOTS * TRIOS)

            def transpose_nodes(base):
                for g in range(-(-NT // 4)):
                    if g >= 2:
                        pe.wait_ge(tr_copied, base + g - 1)
                    for k in range(min(4, NT - 4 * g)):
                        last = pe.transpose((bank_t, bank_h)[g % 2][0:F, k * P:(k + 1) * P], x[:, 4 * g + k, :], ident[:, :])
                    last.then_inc(tr_done, 1)

            def start_sums(lhsT):
                for g, (t0, t1) in enumerate(BANK_TILES):
                    for t in range(t0, t1):
                        lhs, rhs = lhsT(t)
                        pe.matmul(sums[g][:, (t - t0) * W1:(t - t0 + 1) * W1], lhs, rhs,
                                  start=(t == t0), stop=True, skip_group_check=True)

            def merge(slot, done):
                for g, (t0, t1) in enumerate(BANK_TILES):
                    last = pe.matmul(sums[g][:, 0:(t1 - t0) * W1], spread_hot[:, slot, :],
                                     spread[slot][:, t0:t1, :].rearrange("p t f -> p (t f)"),
                                     start=False, stop=True, skip_group_check=True)
                last.then_inc(done, 1)

            def unit_transpose(S, v, k, s, u):
                if u == 0:
                    pe.wait_ge(S.ea_in[s], 16 * (k + 1))
                pe.wait_ge(S.t_copied, 3 * v + u + 1)
                for c, q in enumerate(PAIRS[u]):
                    at = min(2 * q, J - 2) * F
                    last = pe.transpose(bank_t[:, c * P:(c + 1) * P], ea[s][:, at:at + P], ident[:, :])
                last.then_inc(S.t_ready, 1)

            def unit_hidden(S, v, u, first=False):
                n = len(PAIRS[u]) * P
                pe.wait_ge(S.t_copied, 3 * v + u + 2)
                if not first:
                    pe.wait_ge(S.hid_ready, 3 * v + u)
                pe.matmul(bank_h[:, 0:n], mlp1[:, :], eaT[u][:, 0:n], start=True, stop=True)\
                  .then_inc(S.h_ready, 1)

            def unit_out(S, v, u):
                pe.wait_ge(S.hid_ready, 3 * v + u + 1)
                if u == 0:
                    pe.wait_ge(S.mlp_copied, v + 1)
                for c, q in enumerate(PAIRS[u]):
                    at = min(2 * q, J - 2) * F
                    last = pe.matmul(wide[at // 512][:, at % 512:at % 512 + P], hidT[u][:, c * P:(c + 1) * P],
                                     mlp2[:, :], start=True, stop=True)
                last.then_inc(S.unit_done, 1)

            def broadcast(S, v, k, s, n, take, banks):
                if n == 0:
                    pe.wait_ge(S.ends_in[s], 16 * (k + 1))
                pe.wait_ge(S.compared, casts_of(S) * v + n + 1)
                q = n % TRIOS
                chunks = ends_row[s][:, :].rearrange("r (p j) -> r j p", j=J)[:, q * TRIO:(q + 1) * TRIO, :]
                pe.matmul(bank_of(banks, s, n, S)[:, 0:TRIO * P], take[:, :], chunks, start=True, stop=True)\
                  .then_inc(S.broadcast, 1)

            def near_blocks(layer, v0):
                S = near
                looks_up = LOOKED_UP[layer]
                n0 = v0 - NB
                c0 = sum(LOOKED_UP[:layer]) * NB

                def chunk_ends(s, c):
                    return ends_row[s][:, :].rearrange("r (p j) -> r j p", j=J)[:, J - 1 - c, :]

                def cast_act_src(v, k, s):
                    pe.wait_ge(S.ends_in[s], (k + v0 // 2) * 16 + 16)
                    pe.matmul(act_src[s], take_src[:, :], chunk_ends(s, looks_up - 1), start=True, stop=True)\
                      .then_inc(act_src_cast, 1)

                def cast_src(s):
                    for c in range(looks_up - 1):
                        mm = pe.matmul(chunk_src[c], take_src[:, :], chunk_ends(s, c), start=True, stop=True)
                    mm.then_inc(src_cast, 1)

                def find_rows(v, s):
                    for c in range(looks_up):
                        by_act = c == looks_up - 1
                        if by_act:
                            pe.wait_ge(act_lookup_ready, n0 + v + 1)
                        else:
                            pe.wait_ge(lookup_ready, v * (looks_up - 1) + c0 - n0 + c + 1)
                        for t in range(NT):
                            mm = pe.matmul(act_found[s] if by_act else found[c],
                                           (act_lookup if by_act else lookup[c])[:, t, :], x_parts[:, t, :, :].rearrange("p k f -> p (k f)"),
                                           start=(t == 0), stop=(t == NT - 1))
                        mm.then_inc(rows_found, 1)

                if looks_up:
                    cast_act_src(0, 0, 0)
                    cast_src(0)
                    find_rows(0, 0)
                    cast_act_src(1, 0, 1)
                    pe.wait_ge(rows_put, n0 + 1)
                    cast_src(1)

                def body(i, last):
                    for s in range(2):
                        v = 2 * i + s
                        pe.wait_ge(S.hot_ready, v0 + v + 1)
                        before_it = sum(NB // 2 * 16 * gathered(k) for k in range(layer))
                        pe.wait_ge(S.rows_in[s], i * (16 * gathered(layer)) + before_it + 16 * gathered(layer))
                        if looks_up:
                            pe.wait_ge(rows_put, n0 + v + 1)
                        for j in range(J):
                            mm = pe.matmul(part[s], hot[s][:, j, :], rows[s][:, j, :], start=(j == 0), stop=(j == J - 1))
                        mm.then_inc(S.main_done, 1)
                        if looks_up and not (last and s == 1):
                            find_rows(v + 1, 1 - s)
                        if layer == GNN0:
                            for n in (0, 1):
                                broadcast(S, v, i, s, n, take_src, wide)
                        if layer == GNN1:
                            pe.wait_ge(src_hot_ready, v + 1)
                            for j in range(J):
                                mm = pe.matmul(degs, src_hot[s][:, j, :], src_tile[s][:, j, :],
                                               start=False, stop=True, skip_group_check=True)
                            mm.then_inc(src_hot_used, 1)
                        pe.wait_ge(S.spread_ready, v0 + v + 1)
                        if looks_up and not last:
                            cast_act_src(v + 2, i + 1, s)
                        merge(s, S.merged)
                        if layer == GNN0:
                            for n in range(2, TRIOS):
                                broadcast(S, v, i, s, n, take_src, wide)
                        if looks_up and not last:
                            pe.wait_ge(rows_put, n0 + v + 2)
                            cast_src(s)
                blocks(pe, body, looks_up)

            def far_blocks(v0):
                def body(i, last):
                    for s in range(2):
                        for j in range(J):
                            pe.wait_ge(far.spread_ready, (v0 + 2 * i + s) * J + j + 1)
                            merge((s + j) % 2, far.merged)
                blocks(pe, body, False)

            def attend_blocks(S):
                of_dst = casts_of(S) - TRIOS

                def cast(v, k, s, n):
                    if n == of_dst:
                        pe.wait_ge(S.seen_copied, v * TRIOS + SLOTS)
                    broadcast(S, v, k, s, n, take_dst if n < of_dst else take_src, sums[2:4])

                def take(v, k, s, q):
                    if not S.windowed:
                        return
                    if q == 0:
                        pe.wait_ge(S.win_in[s], 16 * (k + 1))
                        pe.wait_ge(S.msg_done, v + 1)
                    pe.wait_ge(S.compared, casts_of(S) * v + q + 1 + SLOTS)
                    for j in range(q * TRIO, (q + 1) * TRIO):
                        for p in range(3):
                            mm = pe.matmul(sums[j // 8][:, j % 8 * F:j % 8 * F + F], dst_hot[s][:, j, :],
                                           win_x[s][:, p * F:(p + 1) * F], start=(p == 0), stop=(p == 2))
                    if q == TRIOS - 1:
                        mm.then_inc(S.taken, 1)

                def sum_same(v, s, after):
                    pe.wait_ge(S.weighted, v + 1)
                    pe.wait_ge(S.compared, after + SLOTS)
                    for q in range(TRIOS):
                        pe.wait_ge(S.seen_copied, v * TRIOS + q + 1)
                        for k in range(TRIO):
                            j = q * TRIO + k
                            for p in range(3):
                                mm = pe.matmul(sums[2 + (s + q) % 2][:, k * W1:(k + 1) * W1], src_same[s][:, j, :],
                                               parts[s][:, p, j, :], start=(p == 0), stop=(p == 2))
                        mm.then_inc(S.seen, 1)

                def body(i, last):
                    for s in range(2):
                        v = 2 * i + s
                        if last and s == 1:
                            for q in range(TRIOS):
                                cast(v, i, s, of_dst + q)
                            sum_same(v, s, casts_of(S) * NB)
                            continue
                        w, k, t = v + 1, i + s, 1 - s

                        def src(*trios):
                            for q in trios:
                                cast(v, i, s, of_dst + q)

                        def dst(*trios):
                            for q in trios:
                                if q < of_dst:
                                    cast(w, k, t, q)

                        src(0, 1)
                        unit_transpose(S, w, k, t, 1)
                        src(2)
                        unit_out(S, w, 0)
                        src(3)
                        unit_hidden(S, w, 1)
                        src(4)
                        unit_transpose(S, w, k, t, 2)
                        dst(0)
                        unit_out(S, w, 1)
                        dst(1)
                        take(w, k, t, 0)
                        unit_hidden(S, w, 2)
                        dst(2)
                        take(w, k, t, 1)
                        dst(3)
                        take(w, k, t, 2)
                        unit_out(S, w, 2)
                        dst(4)
                        take(w, k, t, 3)
                        take(w, k, t, 4)
                        if not last:
                            unit_transpose(S, v + 2, i + 1, s, 0)
                        sum_same(v, s, casts_of(S) * w + of_dst)
                        if not last:
                            unit_hidden(S, v + 2, 0)

                pe.sem_inc(S.broadcast, SLOTS * casts_of(S))
                for n in range(of_dst):
                    cast(0, 0, 0, n)
                for q in range(TRIOS):
                    take(0, 0, 0, q)
                blocks(pe, body, True)

            pe.wait_ge(x_in, 32)
            pe.wait_ge(x_ready, 1)
            transpose_nodes(0)
            pe.wait_ge(first_cast, 1)
            pe.matmul(sums[0][:, 0:NB], ones[0:1, :], first_f[0:1, :], start=True, stop=True).then_inc(first_bc, 1)
            pe.wait_ge(types_in, 48)
            pe.wait_ge(bias_ready, 1)
            pe.wait_ge(tr_copied, -(-NT // 4))
            for t in range(NT):
                pe.wait_ge(prod_used, t + 1)
                pe.matmul(wide[t % 2][:, :], xT[:, t * P:(t + 1) * P], w_types[:, :, :].rearrange("i r o -> i (r o)"),
                          start=True, stop=True).then_inc(prod_done, 1)
            pe.wait_ge(any_col_ready, 1)
            pe.matmul(sums[1][0:1, 0:1], any_col[:, 0:1], ones[:, 0:1], start=True, stop=True).then_inc(any_sum, 1)

            pe.wait_ge(flag_ready, 1)
            start_sums(lambda t: (xT[0:F, t * P:(t + 1) * P], w_loop[:, :]))
            pe.wait_ge(prod_used, 2 + NT)
            near_blocks(GNN0, 0)
            far_way(pe, lambda: far_blocks(0))

            pe.wait_ge(wts_in, 16 * 12)
            pe.wait_ge(x_ready, 2)
            transpose_nodes(-(-NT // 4))
            pe.wait_ge(tr_copied, 2 * -(-NT // 4))
            for g in range(-(-NT // 4)):
                pe.wait_ge(prod_used, NT + g + 1)
                for k in range(min(4, NT - 4 * g)):
                    t = 4 * g + k
                    mm = pe.matmul(wide[g % 2][:, k * F:(k + 1) * F], xT[0:F, t * P:(t + 1) * P], w_gcn[:, :],
                                   start=True, stop=True)
                mm.then_inc(prod_done, 1)
            pe.wait_ge(seed_ready, 1)
            pe.matmul(degs, zero_mat[:, :], iota_tile[:, :], start=True, stop=True, skip_group_check=True)
            start_sums(lambda t: (ident[:, :], seed[:, t, :]))
            near_blocks(GNN1, NB)
            far_way(pe, lambda: far_blocks(NB))

            pe.wait_ge(seed_ready, 2)
            start_sums(lambda t: (ident[:, :], seed[:, t, :]))
            near_blocks(GNN2, 2 * NB)
            far_way(pe, lambda: far_blocks(2 * NB))

            for u in range(len(PAIRS)):
                unit_transpose(attend, 0, 0, 0, u)
                unit_hidden(attend, 0, u, first=(u == 0))
                unit_out(attend, 0, u)
            unit_transpose(attend, 1, 0, 1, 0)
            unit_hidden(attend, 1, 0)
            pe.wait_ge(seed_ready, 3)
            attend_way(pe, attend_blocks)

        @block.vector
        def _(dve):
            steps = [0]

            def step(ins):
                steps[0] += 1
                ins.then_inc(dve_step, 1)
                dve.wait_ge(dve_step, steps[0])

            def rowwise(a):
                return a.unsqueeze(2).to_broadcast([P, NT, F])

            def featurewise(a):
                return a.unsqueeze(1).to_broadcast([P, NT, F])

            roots = [0]

            def inverse_root(a):
                roots[0] += 1
                step(dve.reciprocal(a[:, :], a[:, :]))
                dve.sem_inc(root_in, 1)
                dve.wait_ge(root_done, roots[0])

            def layer_norm(src, dst, mean=stat, var=stat2):
                step(dve.tensor_reduce(mean[:, :], src, axis=AX, op=ALU.add))
                step(dve.tensor_scalar(mean[:, :], mean[:, :], 1.0 / F, None, ALU.mult))
                step(dve.tensor_tensor(xc[:, :, :], src, rowwise(mean[:, :]), ALU.subtract))
                step(dve.tensor_tensor(dst, xc[:, :, :], xc[:, :, :], ALU.mult))
                step(dve.tensor_reduce(var[:, :], dst, axis=AX, op=ALU.add))
                step(dve.tensor_scalar(var[:, :], var[:, :], 1.0 / F, EPS, ALU.mult, ALU.add))
                inverse_root(var)
                step(dve.tensor_tensor(dst, xc[:, :, :], rowwise(var[:, :]), ALU.mult))

            def read_sums(layer, all_near):
                dve.wait_ge(near.merged, SLOTS + all_near)
                far_way(dve, lambda: far_blocks(layer, layer * NB))
                for g, (t0, t1) in enumerate(BANK_TILES):
                    last = dve.tensor_copy(agg[:, t0:t1, :], sums[g][:, 0:(t1 - t0) * W1].rearrange("p (t f) -> p t f", f=W1))
                step(last)

            def edge_scale(layer, s, j, c):
                return weight[:, bass.ds(c, 1)] if layer in (GNN0, GNN1) else None

            def one_hot(out_, numbers, value, scale):
                if scale is None:
                    return dve.tensor_scalar(out_, numbers, value, None, ALU.is_equal)
                return dve.tensor_scalar(out_, numbers, value, scale, ALU.is_equal, ALU.mult)

            def compare_src(S, v, s, n, banks):
                q = n % TRIOS
                dve.wait_ge(S.broadcast, casts_of(S) * (v + SLOTS) + n + 1)
                dve.tensor_tensor(src_same[s][:, q * TRIO:(q + 1) * TRIO, :],
                                  bank_of(banks, s, n, S)[:, 0:TRIO * P].rearrange("p (j e) -> p j e", e=P),
                                  src_f[:, bass.ds(v * J + q * TRIO, TRIO)].unsqueeze(2).to_broadcast([P, TRIO, P]),
                                  ALU.is_equal).then_inc(S.compared, 1)

            def compare_dst(S, v, s, n, banks):
                dve.wait_ge(S.broadcast, casts_of(S) * (v + SLOTS) + n + 1)
                dve.tensor_scalar(dst_hot[s][:, n * TRIO:(n + 1) * TRIO, :].rearrange("p j e -> p (j e)"),
                                  bank_of(banks, s, n, S)[:, 0:TRIO * P], win_f[:, bass.ds(v, 1)], None,
                                  ALU.is_equal).then_inc(S.compared, 1)

            def attend_blocks(S):
                of_dst = casts_of(S) - TRIOS

                def embeddings(v, s):
                    dve.wait_ge(S.unit_done, 3 * v + 9)
                    for g in range(2):
                        n = 8 if g == 0 else J - 8
                        mm = dve.tensor_tensor(mlp_out[s][:, 8 * g:8 * g + n, :],
                                               wide[g][:, 0:n * F].rearrange("p (j f) -> p j f", f=F),
                                               mlp_b2[:, :].unsqueeze(1).to_broadcast([P, n, F]), ALU.add)
                    mm.then_inc(S.mlp_copied, 1)

                def compare(v, s, n):
                    (compare_dst if n < of_dst else compare_src)(S, v, s, n, sums[2:4])

                def body(i, last):
                    for s in range(2):
                        v = 2 * i + s
                        w, t = v + 1, 1 - s
                        dsts = [] if last and s == 1 else list(range(of_dst))
                        dve.wait_ge(S.mlp_copied, v + 2)
                        if S.windowed:
                            dve.wait_ge(S.taken, v + 1)
                            for g in range(2):
                                n = 8 if g == 0 else J - 8
                                mm = dve.tensor_tensor(msg[s][:, 8 * g:8 * g + n, 0:F], mlp_out[s][:, 8 * g:8 * g + n, :],
                                                       sums[g][:, 0:n * F].rearrange("p (j f) -> p j f", f=F), ALU.mult)
                        else:
                            dve.wait_ge(S.rows_in[s], (i + 1) * (16 * J))
                            mm = dve.tensor_tensor(msg[s][:, :, 0:F], mlp_out[s][:, :, :], far_x[s], ALU.mult)
                        mm.then_inc(S.msg_done, 1)
                        dve.wait_ge(S.msg_done, v + 2)
                        dve.tensor_tensor(prod[:, :, :], msg[s][:, :, 0:F],
                                          coef[:, :].unsqueeze(1).to_broadcast([P, J, F]), ALU.mult).then_inc(S.prod_ready, 1)
                        dve.wait_ge(S.prod_ready, v + 1)
                        dve.tensor_reduce(logit[:, s, :], prod[:, :, :], axis=AX, op=ALU.add).then_inc(S.logit_ready, 1)
                        for q in (0, 1):
                            compare(v, s, of_dst + q)
                        dve.wait_ge(S.attn_ready, v + 1)
                        dve.tensor_tensor(weighted[:, :, :], msg[s][:, :, :],
                                          attn[:, s, :].unsqueeze(2).to_broadcast([P, J, W1]), ALU.mult).then_inc(S.part_ready, 1)
                        for q in (2, 3, 4):
                            compare(v, s, of_dst + q)
                        dve.wait_ge(S.part_ready, 2 * v + 1)
                        dve.wait_ge(S.part_cast, 2 * v + 1)
                        dve.tensor_tensor(weighted[:, :, :], weighted[:, :, :], parts[s][:, 0, :, :], ALU.subtract)\
                           .then_inc(S.part_ready, 1)
                        for n in dsts[0:2]:
                            compare(w, t, n)
                        dve.wait_ge(S.part_ready, 2 * v + 2)
                        dve.wait_ge(S.part_cast, 2 * v + 2)
                        dve.tensor_tensor(parts[s][:, 2, :, :], weighted[:, :, :], parts[s][:, 1, :, :], ALU.subtract)\
                           .then_inc(S.weighted, 1)
                        for n in dsts[2:]:
                            compare(w, t, n)
                        if not (last and s == 1):
                            embeddings(w, t)

                for n in range(of_dst):
                    compare(0, 0, n)
                embeddings(0, 0)
                blocks(dve, body, True)

            def table_parts_in_sbuf():
                step(dve.tensor_copy(x_parts[:, :, 0, :], seed[:, :, 0:F]))
                step(dve.tensor_tensor(tmp[:, :, :], seed[:, :, 0:F], x_parts[:, :, 0, :], ALU.subtract))
                step(dve.tensor_copy(x_parts[:, :, 1, :], tmp[:, :, :]))
                step(dve.tensor_tensor(x_parts[:, :, 2, :], tmp[:, :, :], x_parts[:, :, 1, :], ALU.subtract))
                dve.sem_inc(tmp_free, 1)

            def near_blocks(layer, v0):
                S = near
                looks_up = LOOKED_UP[layer]
                n0 = v0 - NB
                c0 = sum(LOOKED_UP[:layer]) * NB

                def look_up(v):
                    dve.wait_ge(src_cast, n0 + v + 1 + SLOTS)
                    for c in range(looks_up - 1):
                        dve.tensor_tensor(lookup[c], chunk_src[c].unsqueeze(1).to_broadcast([P, NT, P]),
                                          node_no[:, :].unsqueeze(2).to_broadcast([P, NT, P]), ALU.is_equal)\
                           .then_inc(lookup_ready, 1)

                def put_rows(v, s):
                    for c in range(looks_up):
                        dve.wait_ge(rows_found, v * looks_up + c0 + c + 1)
                        parts_of = found[c] if c < looks_up - 1 else act_found[s]
                        mm = dve.tensor_reduce(rows[s][:, J - 1 - c, 0:F], parts_of.rearrange("p (k f) -> p f k", k=3),
                                               axis=AX, op=ALU.add)
                    mm.then_inc(rows_put, 1)

                def one_hots(v, s):
                    dve.wait_ge(S.main_done, v0 + v + 1)
                    if layer == GNN2:
                        mm = dve.tensor_tensor(hot[s][:, :, :], iota_row[:, :].unsqueeze(1).to_broadcast([P, J, P]),
                                               rel[:, bass.ds(v * J, J)].unsqueeze(2).to_broadcast([P, J, P]), ALU.is_equal)
                    else:
                        for j in range(J):
                            mm = one_hot(hot[s][:, j, :], iota_row[:, :], rel[:, bass.ds(v * J + j, 1)],
                                         edge_scale(layer, s, j, v * J + j))
                    mm.then_inc(S.hot_ready, 1)

                def body(i, last):
                    for s in range(2):
                        v = 2 * i + s
                        if layer == GNN1:
                            dve.wait_ge(src_hot_used, v + 1)
                            dve.tensor_tensor(src_hot[s][:, :, :], iota_row[:, :].unsqueeze(1).to_broadcast([P, J, P]),
                                              src_lo[:, bass.ds(v * J, J)].unsqueeze(2).to_broadcast([P, J, P]), ALU.is_equal)
                            dve.tensor_tensor(src_tile[s][:, :, :], iota_tile[:, :].unsqueeze(1).to_broadcast([P, J, NT]),
                                              src_hi[:, bass.ds(v * J, J)].unsqueeze(2).to_broadcast([P, J, NT]), ALU.is_equal)\
                               .then_inc(src_hot_ready, 1)
                        if not (last and s == 1):
                            if looks_up:
                                look_up(v + 1)
                            else:
                                one_hots(v + 1, 1 - s)
                        dve.wait_ge(S.merged, v0 + v + 1)
                        one_hot(spread_hot[:, s, :], iota_row[:, :], win_lo[:, bass.ds(v, 1)], None)
                        dve.wait_ge(S.main_done, v0 + v + SLOTS + 1)
                        dve.tensor_tensor(spread[s][:, 0:NT, :], part[s].unsqueeze(1).to_broadcast([P, NT, W1]),
                                          win_mask[:, bass.ds(v, 1), :].rearrange("p b t -> p (b t)").unsqueeze(2)
                                          .to_broadcast([P, NT, W1]), ALU.mult).then_inc(S.spread_ready, 1)
                        if looks_up and not last:
                            one_hots(v + 2, s)
                        if looks_up and not (last and s == 1):
                            put_rows(v + 1, 1 - s)
                        if layer == GNN0:
                            for n in range(TRIOS):
                                dve.wait_ge(S.broadcast, TRIOS * (v + SLOTS) + n + 1)
                                for k in range(TRIO):
                                    c = v * J + n * TRIO + k
                                    mm = dve.scalar_tensor_tensor(
                                        same[s][:, n * TRIO + k, :], bank_of(wide, s, n, S)[:, k * P:(k + 1) * P], src_f[:, bass.ds(c, 1)],
                                        before[:, :], ALU.is_equal, ALU.mult, accum_out=earlier[:, bass.ds(c, 1)])
                                mm.then_inc(S.compared, 1)
                if looks_up:
                    table_parts_in_sbuf()
                one_hots(0, 0)
                if looks_up:
                    one_hots(1, 1)
                    look_up(0)
                    put_rows(0, 0)
                if layer == GNN0:
                    for g in range(2):
                        dve.wait_ge(landed[g], 16 * TRIO)
                blocks(dve, body, True)

            def far_blocks(layer, v0):
                S = far

                def body(i, last):
                    for s in range(2):
                        v = 2 * i + s
                        dve.wait_ge(S.rows_in[s], (i + v0 // 2) * (16 * J) + 16 * J)
                        for j in range(J):
                            q = (s + j) % 2
                            g = (v0 + v) * J + j
                            dve.wait_ge(S.merged, g + FAR_SLOTS - 1)
                            dve.tensor_scalar(far_mask[:, q, :], iota_tile[:, :], far_hi[:, bass.ds(v * J + j, 1)],
                                              None, ALU.is_equal).then_inc(S.mask_done, 1)
                            one_hot(spread_hot[:, q, :], iota_row[:, :], far_lo[:, bass.ds(v * J + j, 1)],
                                    edge_scale(layer, s, j, v * J + j))
                            dve.wait_ge(S.mask_done, g + 1)
                            dve.tensor_tensor(spread[q][:, 0:NT, :],
                                              rows[s][:, j, :].unsqueeze(1).to_broadcast([P, NT, W1]),
                                              far_mask[:, q, :].unsqueeze(2).to_broadcast([P, NT, W1]), ALU.mult)\
                               .then_inc(S.spread_ready, 1)
                blocks(dve, body, False)
                dve.wait_ge(S.merged, FAR_SLOTS + (v0 + NB) * J)

            dve.sem_inc(attend.msg_done, 1)
            dve.sem_inc(attend.mlp_copied, 1)
            dve.sem_inc(attend.t_copied, 1)
            dve.sem_inc(attend.seen_copied, SLOTS)
            for S in (near, attend):
                dve.sem_inc(S.compared, SLOTS)
            dve.sem_inc(prod_used, 2)
            dve.memset(x[:, NT - 1, :], 0.0)
            dve.memset(mlp1[:, :], 0.0)
            dve.memset(mlp2[:, :], 0.0).then_inc(zeroed, 1)
            dve.memset(w_loop[:, F:W1], 0.0)
            dve.memset(zero_mat[:, :], 0.0)
            dve.memset(spread[0][:, :, :], 0.0).then_inc(cleared, 1)
            for s in range(2):
                dve.memset(rows[s][:, :, F:W1], 1.0)
                dve.memset(msg[s][:, :, F:W1], 1.0)
            step(dve.memset(ones[:, :], 1.0))
            dve.wait_ge(consts, 3)
            step(dve.tensor_scalar(ident[:, :], iota_row[:, :], row_no[:, 0:1], None, ALU.is_equal))
            dve.sem_inc(x_ready, 1)
            dve.memset(xT[F:F + 1, :], 1.0)
            dve.memset(repeated[0], -1.0)
            step(dve.memset(repeated[1], 0.0))
            step(dve.tensor_scalar(node_no[:, :], iota_tile[:, :], float(P), None, ALU.mult))
            step(dve.tensor_scalar(node_no[:, :], node_no[:, :], row_no[:, 0:1], None, ALU.add))
            step(dve.tensor_scalar(before[:, :], iota_row[:, :], row_no[:, 0:1], None, ALU.is_lt))
            step(dve.tensor_scalar(take_dst[:, :], ones[0:4, :], row_no[0:4, 0:1], 2.0, ALU.mult, ALU.is_ge))
            step(dve.tensor_scalar(take_src[:, :], ones[0:4, :], row_no[0:4, 0:1], 2.0, ALU.mult, ALU.is_lt))
            dve.wait_ge(types_in, 48)
            dve.tensor_copy(w_types[F:F + 1, :, :], h_bias[F:F + 1, :].unsqueeze(1).to_broadcast([1, R, F])).then_inc(bias_ready, 1)

            def cast_ends(n):
                dve.wait_ge(ends_loaded, 32 * (n + 1))
                if n:
                    dve.wait_ge(ends_out, 16 * 6 * n)
                step(dve.tensor_copy(ends_ab[0], ends_i))
                dve.tensor_tensor(ends_ab[1], ends_i, ends_ab[0], ALU.subtract).then_inc(ends_cast, 1)

            dve.wait_ge(dst_in, 32)
            step(dve.tensor_copy(first_f[0:1, :], dst_i[0:1, :].rearrange("p (b j) -> p b j", j=J)[:, :, 0]))
            dve.sem_inc(first_cast, 1)
            cast_ends(0)
            dve.wait_ge(src_in, 64)
            step(dve.tensor_scalar(tmp_i[:, :], src_i[:, :], float(R), None, ALU.mult))
            dve.tensor_tensor(typed_i[:, :], tmp_i[:, :], type_i[:, :], ALU.add).then_inc(idx0_ready, 1)
            dve.wait_ge(first_bc, 1)
            step(dve.tensor_copy(first[:, :], sums[0][:, 0:NB]))
            step(dve.tensor_scalar(win_i[:, :], first[:, :], row_no[:, 0:1], None, ALU.add))
            per_block = first[:, :].unsqueeze(2).to_broadcast([P, NB, J])
            step(dve.tensor_tensor(rel[:, :].rearrange("p (b j) -> p b j", j=J),
                                   dst_i[:, :].rearrange("p (b j) -> p b j", j=J), per_block, ALU.subtract))
            step(dve.tensor_single_scalar(win_t[:, :], win_i[:, :], P - 1, ALU.bitwise_and))
            step(dve.tensor_copy(win_lo[:, :], win_t[:, :]))
            step(dve.tensor_copy(win_f[:, :], win_i[:, :]))
            step(dve.tensor_single_scalar(win_t[:, :], win_i[:, :], 7, ALU.arith_shift_right))
            step(dve.tensor_copy(win_hi[:, :], win_t[:, :]))
            step(dve.tensor_tensor(win_mask[:, :, :], iota_tile[:, :].unsqueeze(1).to_broadcast([P, NB, NT]),
                                   win_hi[:, :].unsqueeze(2).to_broadcast([P, NB, NT]), ALU.is_equal))
            step(dve.tensor_scalar(inside[:, :], rel[:, :], 0.0, None, ALU.is_ge))
            step(dve.tensor_scalar(outside[:, :], rel[:, :], float(WINDOW), None, ALU.is_lt))
            step(dve.tensor_tensor(inside[:, :], inside[:, :], outside[:, :], ALU.mult))
            step(dve.tensor_scalar(outside[:, :], inside[:, :], -1.0, 1.0, ALU.mult, ALU.add))
            step(dve.memset(outside[0:REPEATED, (NB - 1) * J:], 0.0))
            step(dve.tensor_reduce(any_col[:, :], outside[:, :], axis=AX, op=ALU.add))
            dve.sem_inc(any_col_ready, 1)
            cast_ends(1)
            step(dve.tensor_scalar(rel[:, :], rel[:, :], 1.0, None, ALU.add))
            step(dve.tensor_tensor(rel[:, :], rel[:, :], inside[:, :], ALU.mult))
            step(dve.tensor_scalar(rel[:, :], rel[:, :], -1.0, None, ALU.add))
            step(dve.memset(rel[0:REPEATED, (NB - 1) * J:], -1.0))
            step(dve.tensor_single_scalar(tmp_i[:, :], dst_i[:, :], P - 1, ALU.bitwise_and))
            step(dve.tensor_copy(far_lo[:, :], tmp_i[:, :]))
            step(dve.tensor_single_scalar(tmp_i[:, :], dst_i[:, :], 7, ALU.arith_shift_right))
            step(dve.tensor_copy(far_hi[:, :], tmp_i[:, :]))
            step(dve.tensor_scalar(far_hi[:, :], far_hi[:, :], 1.0, None, ALU.add))
            step(dve.tensor_tensor(far_hi[:, :], far_hi[:, :], outside[:, :], ALU.mult))
            step(dve.tensor_scalar(far_hi[:, :], far_hi[:, :], -1.0, None, ALU.add))
            step(dve.tensor_single_scalar(tmp_i[:, :], src_i[:, :], P - 1, ALU.bitwise_and))
            step(dve.tensor_copy(src_lo[:, :], tmp_i[:, :]))
            step(dve.tensor_single_scalar(tmp_i[:, :], src_i[:, :], 7, ALU.arith_shift_right))
            step(dve.tensor_copy(src_hi[:, :], tmp_i[:, :]))
            step(dve.tensor_copy(src_f[:, :], src_i[:, :]))
            step(dve.memset(src_f[0:REPEATED, (NB - 1) * J:], -1.0))
            step(dve.memset(src_hi[0:REPEATED, (NB - 1) * J:], -1.0))
            dve.wait_ge(any_sum, 1)
            step(dve.tensor_copy(any_i[0:1, :], sums[1][0:1, 0:1]))
            dve.sem_inc(flag_ready, 1)
            dve.wait_ge(w_in, 32)
            dve.wait_ge(wts_in, 16 * 12)
            dve.wait_ge(x_in, 32)
            dve.wait_ge(ends_out, 16 * 12)

            near_blocks(GNN0, 0)
            read_sums(GNN0, NB)
            step(dve.tensor_tensor(tmp[:, :, :], x[:, :, :], agg[:, :, 0:F], ALU.add))
            layer_norm(tmp[:, :, :], x[:, :, :])
            dve.sem_inc(x_ready, 1)
            step(dve.tensor_scalar(stat[:, :], agg[:, :, F], 1.0, None, ALU.add))
            step(dve.tensor_scalar(stat2[:, :], stat[:, :], 0.0, None, ALU.is_gt))
            step(dve.tensor_scalar(dinv[:, :], stat[:, :], 1e-37, None, ALU.max))
            inverse_root(dinv)
            step(dve.tensor_tensor(dinv[:, :], dinv[:, :], stat2[:, :], ALU.mult))

            step(dve.memset(seed[:, :, F:W1], 1.0))
            for g in range(-(-NT // 4)):
                n = min(4, NT - 4 * g)
                dve.wait_ge(prod_done, NT + g + 1)
                dve.tensor_tensor(seed[:, 4 * g:4 * g + n, 0:F], wide[g % 2][:, 0:n * F].rearrange("p (t f) -> p t f", f=F),
                                  dinv[:, 4 * g:4 * g + n].unsqueeze(2).to_broadcast([P, n, F]), ALU.mult)\
                   .then_inc(prod_used, 1)
            dve.wait_ge(prod_used, 2 + NT + -(-NT // 4))
            dve.sem_inc(table_ready, 1)
            dve.sem_inc(seed_ready, 1)
            near_blocks(GNN1, NB)
            read_sums(GNN1, 2 * NB)
            step(dve.tensor_scalar(deg_out[:, :], degs, 1.0, None, ALU.add))
            step(dve.tensor_tensor(tmp[:, :, :], agg[:, :, 0:F], rowwise(dinv[:, :]), ALU.mult))
            step(dve.tensor_tensor(tmp[:, :, :], tmp[:, :, :], featurewise(g_bias[:, :]), ALU.add))
            layer_norm(tmp[:, :, :], agg[:, :, 0:F])
            step(dve.tensor_tensor(tmp[:, :, :], agg[:, :, 0:F], featurewise(gamma[:, :]), ALU.mult))
            step(dve.tensor_tensor(tmp[:, :, :], tmp[:, :, :], featurewise(beta[:, :]), ALU.add))
            dve.sem_inc(gelu_in, 1)
            dve.wait_ge(gelu_done, 1)
            step(dve.tensor_tensor(tmp[:, :, :], x[:, :, :], xc[:, :, :], ALU.add))
            layer_norm(tmp[:, :, :], x[:, :, :])

            dve.wait_ge(table_out, 32)
            step(dve.tensor_scalar(stat[:, :], deg_out[:, :], 1.0, None, ALU.max))
            inverse_root(stat)
            step(dve.tensor_tensor(seed[:, :, 0:F], x[:, :, :], rowwise(stat[:, :]), ALU.mult))
            dve.sem_inc(table_ready, 1)
            dve.sem_inc(seed_ready, 1)
            step(dve.tensor_scalar(earlier[:, :], earlier[:, :], 0.0, None, ALU.is_equal))
            step(dve.memset(earlier[0:REPEATED, (NB - 1) * J:], 0.0))
            step(dve.tensor_scalar(stat2[:, 0:1], row_no[:, 0:1], float(SLOT_ROWS), float(NT), ALU.mult, ALU.add))
            step(dve.tensor_scalar(outside[:, :], src_lo[:, :], float(SLOT_ROWS), None, ALU.mult))
            step(dve.tensor_tensor(outside[:, :], outside[:, :], src_hi[:, :], ALU.add))
            step(dve.tensor_scalar(outside[:, :], outside[:, :], stat2[:, 0:1], None, ALU.subtract))
            step(dve.tensor_tensor(outside[:, :], outside[:, :], earlier[:, :], ALU.mult))
            step(dve.tensor_scalar(scat_i[:, :], outside[:, :], stat2[:, 0:1], None, ALU.add))
            dve.sem_inc(scatter_ready, 1)

            near_blocks(GNN2, 2 * NB)
            read_sums(GNN2, 3 * NB)
            step(dve.tensor_scalar(stat[:, :], agg[:, :, F], 1.0, None, ALU.max))
            inverse_root(stat)
            step(dve.tensor_tensor(tmp[:, :, :], agg[:, :, 0:F], rowwise(stat[:, :]), ALU.mult))
            step(dve.tensor_tensor(tmp[:, :, :], tmp[:, :, :], x[:, :, :], ALU.add))
            layer_norm(tmp[:, :, :], x[:, :, :])

            dve.sem_inc(table_ready, 1)
            dve.sem_inc(seed_ready, 1)
            dve.wait_ge(hi_ready, 1)
            step(dve.tensor_tensor(tmp[:, :, :], x[:, :, :], x_parts[:, :, 0, :], ALU.subtract))
            dve.sem_inc(rest_ready, 1)
            dve.wait_ge(mid_ready, 1)
            step(dve.tensor_tensor(x_parts[:, :, 2, :], tmp[:, :, :], x_parts[:, :, 1, :], ALU.subtract))
            dve.sem_inc(parts_ready, 1)
            dve.wait_ge(table_out, 64)
            attend_way(dve, attend_blocks)
            dve.wait_ge(parts_out, 48)
            for k in range(TRIO):
                dve.wait_ge(final_in[k], 32)
                step(dve.tensor_tensor(finals[k][:, 0:NT, :], finals[k][:, 0:NT, :], finals[k + TRIO][:, 0:NT, :], ALU.add))
            step(dve.tensor_tensor(finals[0][:, 0:NT, :], finals[0][:, 0:NT, :], finals[1][:, 0:NT, :], ALU.add))
            step(dve.tensor_tensor(agg[:, :, :], finals[0][:, 0:NT, :], finals[2][:, 0:NT, :], ALU.add))
            step(dve.tensor_scalar(stat[:, :], agg[:, :, F], 0.0, None, ALU.is_gt))
            step(dve.tensor_scalar(stat2[:, :], stat[:, :], -1.0, 1.0, ALU.mult, ALU.add))
            step(dve.tensor_tensor(stat[:, :], stat[:, :], agg[:, :, F], ALU.mult))
            step(dve.tensor_tensor(stat[:, :], stat[:, :], stat2[:, :], ALU.add))
            step(dve.reciprocal(stat[:, :], stat[:, :]))
            step(dve.tensor_tensor(tmp[:, :, :], agg[:, :, 0:F], rowwise(stat[:, :]), ALU.mult))
            step(dve.tensor_tensor(tmp[:, :, :], tmp[:, :, :], x[:, :, :], ALU.add))
            layer_norm(tmp[:, :, :], x[:, :, :])
            dve.sem_inc(table_ready, 1)


INPUTS = ["x", "src", "dst", "edge_attr_64", "edge_type_8", "edge_weight1", "L0_gnn_weight", "L0_gnn_h_bias",
          "L0_gnn_loop_weight", "L1_gnn_W", "L1_gnn_b", "L1_gnn_gamma", "L1_gnn_beta", "L3_gnn_W1", "L3_gnn_b1",
          "L3_gnn_W2", "L3_gnn_b2", "L3_gnn_linear_coef"]


def kernel(**inputs):
    import numpy as np
    import concourse.bacc as bacc
    from concourse.bass_utils import run_bass_kernel_spmd

    nc = bacc.Bacc("TRN2", target_bir_lowering=False, num_devices=1)
    arrays, A = {}, {}
    for name in INPUTS:
        a = np.ascontiguousarray(inputs[name])
        arrays["in_" + name] = a
        A[name] = nc.dram_tensor("in_" + name, a.shape, mybir.dt.from_np(a.dtype), kind="ExternalInput").ap()
    out = nc.dram_tensor("out_0", (N, F), F32, kind="ExternalOutput").ap()
    build(nc, A, out)
    result = run_bass_kernel_spmd(nc, [arrays], core_ids=[0])
    return result.results[0]["out_0"]
```
